# Optimizing a Trainium2 kernel written in Bass

```python
import numpy as np
import jax
import jax.numpy as jnp

def _softmax(x, axis=-1):
    return jax.nn.softmax(x, axis=axis)

def _gelu(x):
    return jax.nn.gelu(x, approximate=True)

def _silu(x):
    return jax.nn.silu(x)

def _sigmoid(x):
    return jax.nn.sigmoid(x)

def _layernorm(x, axis=-1, eps=1e-05):
    m = jnp.mean(x, axis=axis, keepdims=True)
    v = jnp.var(x, axis=axis, keepdims=True)
    return (x - m) / jnp.sqrt(v + eps)

def _scatter_add(tgt, idx, src, axis=0):
    return tgt.at[idx].add(src)

def _segment_sum(src, seg, n):
    return jax.ops.segment_sum(src, seg, n)
kernel_name = 'mk_macaron_d1_jaxref_r8_44e826'

def setup_inputs(seed: int=0):
    np.random.seed(seed)
    _w = jnp.asarray

    def _L0_attn_setup():
        import jax, jax.numpy as jnp
        import numpy as np
        N_HEAD = 16
        ROPE_BASE = 10000.0

        def _rope(Y, d_param):
            b, h, t, dh = Y.shape
            mid = d_param // 2
            Y1 = Y[:, :mid]
            Y2 = Y[:, mid:]
            Ym1 = jnp.concatenate([Y1, Y2], axis=1)
            Ym2 = jnp.concatenate([-Y2, Y1], axis=1)
            j = jnp.arange(t, dtype=Y.dtype)[:, None]
            i = jnp.arange(dh // 2, dtype=Y.dtype)[None, :]
            theta = j * jnp.power(jnp.asarray(ROPE_BASE, Y.dtype), -2.0 * i / dh)
            cos = jnp.cos(theta)
            sin = jnp.sin(theta)
            theta1 = jnp.concatenate([cos, cos], axis=1)
            theta2 = jnp.concatenate([sin, sin], axis=1)
            return Ym1 * theta1 + Ym2 * theta2
        key = jax.random.key(seed)
        ks = jax.random.split(key, 9)
        b, t, e = (2, 256, 128)
        s = 1.0 / np.sqrt(e)
        return {'x': jax.random.normal(ks[0], (b, t, e), dtype=jnp.float32), 'Wq': jax.random.normal(ks[1], (e, e), dtype=jnp.float32) * s, 'bq': jax.random.normal(ks[2], (e,), dtype=jnp.float32) * 0.01, 'Wk': jax.random.normal(ks[3], (e, e), dtype=jnp.float32) * s, 'bk': jax.random.normal(ks[4], (e,), dtype=jnp.float32) * 0.01, 'Wv': jax.random.normal(ks[5], (e, e), dtype=jnp.float32) * s, 'bv': jax.random.normal(ks[6], (e,), dtype=jnp.float32) * 0.01, 'Wo': jax.random.normal(ks[7], (e, e), dtype=jnp.float32) * s, 'bo': jax.random.normal(ks[8], (e,), dtype=jnp.float32) * 0.01}
    _L0_attn_in = _L0_attn_setup()

    def _L0_ffn_setup():
        import jax, jax.numpy as jnp
        import numpy as np
        D = 128
        H = 16
        KV = 8
        HD = D // H
        M = 448
        E = 8
        TOPK = 2
        EPS = 1e-06
        ROPE_THETA = 10000.0

        def _rmsnorm(x, w, eps=EPS):
            xf = x.astype(jnp.float32)
            var = jnp.mean(xf * xf, axis=-1, keepdims=True)
            return (xf * jax.lax.rsqrt(var + eps)).astype(x.dtype) * w

        def _rope(q, k):
            S = q.shape[1]
            inv_freq = 1.0 / ROPE_THETA ** (jnp.arange(0, HD, 2, dtype=jnp.float32) / HD)
            ang = jnp.arange(S, dtype=jnp.float32)[:, None] * inv_freq[None, :]
            cos = jnp.concatenate([jnp.cos(ang), jnp.cos(ang)], axis=-1)[None, :, None, :]
            sin = jnp.concatenate([jnp.sin(ang), jnp.sin(ang)], axis=-1)[None, :, None, :]

            def rot_half(t):
                t1, t2 = jnp.split(t, 2, axis=-1)
                return jnp.concatenate([-t2, t1], axis=-1)
            return (q * cos + rot_half(q) * sin, k * cos + rot_half(k) * sin)
        key = jax.random.key(seed)
        ks = jax.random.split(key, 12)
        s = 0.02
        B, S = (2, 128)
        return {'x': jax.random.normal(ks[0], (B, S, D), jnp.float32), 'ln1_w': jnp.ones((D,), jnp.float32), 'ln2_w': jnp.ones((D,), jnp.float32), 'wq': jax.random.normal(ks[1], (D, H * HD), jnp.float32) * s, 'wk': jax.random.normal(ks[2], (D, KV * HD), jnp.float32) * s, 'wv': jax.random.normal(ks[3], (D, KV * HD), jnp.float32) * s, 'wo': jax.random.normal(ks[4], (H * HD, D), jnp.float32) * s, 'router_w': jax.random.normal(ks[5], (D, E), jnp.float32) * s, 'w_gate': jax.random.normal(ks[6], (E, D, M), jnp.float32) * s, 'w_up': jax.random.normal(ks[7], (E, D, M), jnp.float32) * s, 'w_down': jax.random.normal(ks[8], (E, M, D), jnp.float32) * s}
    _L0_ffn_in = _L0_ffn_setup()
    _d = {'L0_attn_x': _L0_attn_in['x'], 'L0_attn_Wq': _L0_attn_in['Wq'], 'L0_attn_bq': _L0_attn_in['bq'], 'L0_attn_Wk': _L0_attn_in['Wk'], 'L0_attn_bk': _L0_attn_in['bk'], 'L0_attn_Wv': _L0_attn_in['Wv'], 'L0_attn_bv': _L0_attn_in['bv'], 'L0_attn_Wo': _L0_attn_in['Wo'], 'L0_attn_bo': _L0_attn_in['bo'], 'L0_ffn_ln1_w': _L0_ffn_in['ln1_w'], 'L0_ffn_ln2_w': _L0_ffn_in['ln2_w'], 'L0_ffn_wq': _L0_ffn_in['wq'], 'L0_ffn_wk': _L0_ffn_in['wk'], 'L0_ffn_wv': _L0_ffn_in['wv'], 'L0_ffn_wo': _L0_ffn_in['wo'], 'L0_ffn_router_w': _L0_ffn_in['router_w'], 'L0_ffn_w_gate': _L0_ffn_in['w_gate'], 'L0_ffn_w_up': _L0_ffn_in['w_up'], 'L0_ffn_w_down': _L0_ffn_in['w_down']}
    _x0 = _d['L0_attn_x']
    _d['L0_attn_x'] = jax.random.normal(jax.random.fold_in(jax.random.key(seed), 1), (1, 2048, 128), dtype=_x0.dtype)
    del _x0
    return _d

def reference(L0_attn_x, L0_attn_Wq, L0_attn_bq, L0_attn_Wk, L0_attn_bk, L0_attn_Wv, L0_attn_bv, L0_attn_Wo, L0_attn_bo, L0_ffn_ln1_w, L0_ffn_ln2_w, L0_ffn_wq, L0_ffn_wk, L0_ffn_wv, L0_ffn_wo, L0_ffn_router_w, L0_ffn_w_gate, L0_ffn_w_up, L0_ffn_w_down):

    def _L0_attn_ref(x, Wq, bq, Wk, bk, Wv, bv, Wo, bo):
        import jax, jax.numpy as jnp
        import numpy as np
        N_HEAD = 16
        ROPE_BASE = 10000.0

        def _rope(Y, d_param):
            b, h, t, dh = Y.shape
            mid = d_param // 2
            Y1 = Y[:, :mid]
            Y2 = Y[:, mid:]
            Ym1 = jnp.concatenate([Y1, Y2], axis=1)
            Ym2 = jnp.concatenate([-Y2, Y1], axis=1)
            j = jnp.arange(t, dtype=Y.dtype)[:, None]
            i = jnp.arange(dh // 2, dtype=Y.dtype)[None, :]
            theta = j * jnp.power(jnp.asarray(ROPE_BASE, Y.dtype), -2.0 * i / dh)
            cos = jnp.cos(theta)
            sin = jnp.sin(theta)
            theta1 = jnp.concatenate([cos, cos], axis=1)
            theta2 = jnp.concatenate([sin, sin], axis=1)
            return Ym1 * theta1 + Ym2 * theta2
        b, t, e = x.shape
        h = N_HEAD
        dh = e // h

        def proj(W, bias):
            y = jnp.einsum('bte,fe->btf', x, W) + bias
            return y.reshape(b, t, h, dh).transpose(0, 2, 1, 3)
        q = _rope(proj(Wq, bq), e)
        k = _rope(proj(Wk, bk), e)
        v = proj(Wv, bv)
        scale = jnp.sqrt(jnp.asarray(dh, x.dtype))
        att = jnp.einsum('bhqd,bhkd->bhqk', q, k) / scale
        causal = jnp.tril(jnp.ones((t, t), dtype=bool))
        att = jnp.where(causal[None, None], att, -jnp.inf)
        att = jax.nn.softmax(att, axis=-1)
        y = jnp.einsum('bhqk,bhkd->bhqd', att, v)
        y = y.transpose(0, 2, 1, 3).reshape(b, t, e)
        return jnp.einsum('bte,fe->btf', y, Wo) + bo

    def _L0_ffn_ref(x, ln1_w, ln2_w, wq, wk, wv, wo, router_w, w_gate, w_up, w_down):
        import jax, jax.numpy as jnp
        import numpy as np
        D = 128
        H = 16
        KV = 8
        HD = D // H
        M = 448
        E = 8
        TOPK = 2
        EPS = 1e-06
        ROPE_THETA = 10000.0

        def _rmsnorm(x, w, eps=EPS):
            xf = x.astype(jnp.float32)
            var = jnp.mean(xf * xf, axis=-1, keepdims=True)
            return (xf * jax.lax.rsqrt(var + eps)).astype(x.dtype) * w

        def _rope(q, k):
            S = q.shape[1]
            inv_freq = 1.0 / ROPE_THETA ** (jnp.arange(0, HD, 2, dtype=jnp.float32) / HD)
            ang = jnp.arange(S, dtype=jnp.float32)[:, None] * inv_freq[None, :]
            cos = jnp.concatenate([jnp.cos(ang), jnp.cos(ang)], axis=-1)[None, :, None, :]
            sin = jnp.concatenate([jnp.sin(ang), jnp.sin(ang)], axis=-1)[None, :, None, :]

            def rot_half(t):
                t1, t2 = jnp.split(t, 2, axis=-1)
                return jnp.concatenate([-t2, t1], axis=-1)
            return (q * cos + rot_half(q) * sin, k * cos + rot_half(k) * sin)
        B, S, _ = x.shape
        h = _rmsnorm(x, ln1_w)
        q = (h @ wq).reshape(B, S, H, HD)
        k = (h @ wk).reshape(B, S, KV, HD)
        v = (h @ wv).reshape(B, S, KV, HD)
        q, k = _rope(q, k)
        rep = H // KV
        k = jnp.repeat(k, rep, axis=2)
        v = jnp.repeat(v, rep, axis=2)
        scores = jnp.einsum('bqhd,bkhd->bhqk', q, k) / jnp.sqrt(jnp.float32(HD))
        causal = jnp.tril(jnp.ones((S, S), bool))
        scores = jnp.where(causal[None, None], scores, jnp.finfo(scores.dtype).min)
        attn = jax.nn.softmax(scores, axis=-1)
        ao = jnp.einsum('bhqk,bkhd->bqhd', attn, v).reshape(B, S, H * HD)
        x = x + ao @ wo
        h = _rmsnorm(x, ln2_w)
        logits = h @ router_w
        probs = jax.nn.softmax(logits, axis=-1)
        topv, topi = jax.lax.top_k(probs, TOPK)
        topv = topv / jnp.sum(topv, axis=-1, keepdims=True)
        weights = jnp.sum(jax.nn.one_hot(topi, E, dtype=h.dtype) * topv[..., None], axis=-2)
        gate = jnp.einsum('bsd,edm->bsem', h, w_gate)
        up = jnp.einsum('bsd,edm->bsem', h, w_up)
        act = jax.nn.silu(gate) * up * weights[..., None]
        moe = jnp.einsum('bsem,emd->bsd', act, w_down)
        return x + moe
    x = L0_attn_x
    x = x + 0.5 * _L0_ffn_ref(_layernorm(x, axis=-1), L0_ffn_ln1_w, L0_ffn_ln2_w, L0_ffn_wq, L0_ffn_wk, L0_ffn_wv, L0_ffn_wo, L0_ffn_router_w, L0_ffn_w_gate, L0_ffn_w_up, L0_ffn_w_down)
    x = x + _L0_attn_ref(_layernorm(x, axis=-1), L0_attn_Wq, L0_attn_bq, L0_attn_Wk, L0_attn_bk, L0_attn_Wv, L0_attn_bv, L0_attn_Wo, L0_attn_bo)
    x = x + 0.5 * _L0_ffn_ref(_layernorm(x, axis=-1), L0_ffn_ln1_w, L0_ffn_ln2_w, L0_ffn_wq, L0_ffn_wk, L0_ffn_wv, L0_ffn_wo, L0_ffn_router_w, L0_ffn_w_gate, L0_ffn_w_up, L0_ffn_w_down)
    return x

_drawn_inputs = setup_inputs


def setup_inputs(seed=0):
    import zlib

    import numpy as np

    out = dict(_drawn_inputs(seed))
    spreads = {'L0_ffn_ln1_w': (1.0, 0.6), 'L0_ffn_ln2_w': (1.0, 0.6)}
    factors = {'L0_attn_bq': 8.0,
     'L0_attn_bk': 8.0,
     'L0_attn_bv': 7.848,
     'L0_attn_bo': 8.0,
     'L0_ffn_wq': 8.0,
     'L0_ffn_wk': 8.0,
     'L0_ffn_wv': 8.0,
     'L0_ffn_wo': 8.0,
     'L0_ffn_router_w': 8.0,
     'L0_ffn_w_gate': 8.0,
     'L0_ffn_w_up': 8.0,
     'L0_ffn_w_down': 8.0}
    for name, (base, spread) in spreads.items():
        noise = np.random.default_rng([zlib.crc32(name.encode()), seed]).standard_normal(out[name].shape)
        drawn = base * np.exp(spread * noise) if base else spread * noise
        out[name] = jnp.asarray(drawn.astype(out[name].dtype))
    for name, factor in factors.items():
        out[name] = (out[name] * factor).astype(out[name].dtype)
    return out
```

```python
import numpy as np
import concourse.bass as bass
from concourse import mybir

F32 = mybir.dt.float32
BF16 = mybir.dt.bfloat16
ALU = mybir.AluOpType
ACT = mybir.ActivationFunctionType
AX = mybir.AxisListType

T, D = 2048, 128
TT = T // 128
H, HD = 16, 8
HPG = 4
NG = H // HPG
CH = 512
NC = T // CH
TPC = CH // 128
KROWS = 96
GUARD = 9 * HD
E, M = 8, 448
MC, MR = 4, 112
NLAYER = 3
SCALE = float(1.0 / np.sqrt(np.float32(HD)))
MASKED = -1e30
LN_EPS, RMS_EPS = 1e-5, 1e-6
W_Q, W_QR, W_K, W_KR, W_V = range(5)
V_LN1, V_BV, V_BO, V_LN2 = range(4)


def core_schedule():
    chunks = []
    for g in range(NG):
        cs = list(range(NC))
        chunks += [(g, c) for c in (cs if g % 2 == 0 else cs[::-1])]
    maxima, due = [], []
    for j, (g, c) in enumerate(chunks):
        units = [("rowmax", j, qt, h, kc) for qt in range(TPC) for h in range(HPG) for kc in range(c + 1)]
        if j:
            units.insert(2, ("maxout", j - 1))
        maxima += units
        due.append(len(maxima))
    maxima.append(("maxout", len(chunks) - 1))
    due = [min(d + 3, len(maxima)) for d in due]
    steps = [(j, kt) for j, (g, c) in enumerate(chunks) for kt in range(TPC * (c + 1))]
    total = len(steps)
    events, done = [], 0
    start_of = {}
    for s, (j, kt) in enumerate(steps):
        start_of.setdefault(j, s)
    need = [0] * (total + 1)
    ahead = 5
    for j in range(len(chunks)):
        need[max(0, start_of[j] - (ahead if j else 0))] = max(due[j], need[max(0, start_of[j] - ahead)])
    want = [0] * total
    level = 0.0
    for s in range(total):
        rate = 0.0
        if need[s] > level:
            level = need[s]
        for j in range(len(chunks)):
            at = start_of[j] - ahead
            if at > s and due[j] > level:
                rate = max(rate, (due[j] - level) / (at - s))
        want[s] = int(np.ceil(level))
        level = min(len(maxima), level + rate)
    for s, (j, kt) in enumerate(steps):
        todo = max(0, min(want[s], len(maxima)) - done)
        gap = []
        for slot in range(4):
            k = (todo + 3 - slot) // 4
            gap.append(maxima[done:done + k])
            done += k
        if s == 0:
            for k in range(4):
                events += gap[k]
                gap[k] = []
        events.append(("scores", s, j, kt, 0))
        events += gap[0]
        events.append(("scores", s, j, kt, 1))
        events += gap[1]
        if s:
            pj, pk = steps[s - 1]
            events.append(("values", s - 1, pj, pk))
            if pj != j:
                events.append(("evacuate", pj))
        events += gap[2]
        if j and kt == 2:
            events.append(("normalise", j - 1))
        events += gap[3]
        if kt == TPC * (chunks[j][1] + 1) - 1 and chunks[j][1] == (NC - 1 if chunks[j][0] % 2 == 0 else 0):
            events.append(("reload", chunks[j][0]))
    while done < len(maxima):
        events.append(maxima[done])
        done += 1
    j = len(chunks) - 1
    events.append(("values", total - 1, j, steps[-1][1]))
    events.append(("evacuate", j))
    events.append(("normalise", j))
    return chunks, events


def macaron_kernel(nc, x_in, w5, b4, vecs, wo_w, rope, router, w_gate, w_up, w_down, out):
    def sb(name, shape, dt=F32):
        return nc.alloc_sbuf_tensor(name, shape, dt)

    xs = sb("xs", [128, TT, D])
    x1 = sb("x1", [128, TT, D])
    hT = sb("hT", [128, T])
    qa = sb("qa", [128, 2, HPG, T], BF16)
    ka = sb("ka", [128, 2, HPG, T], BF16)
    vv = sb("vv", [128, TT, H, HD + 1])
    probs = sb("probs", [128, 2, HPG, CH])
    rtab = probs[:, :, :, :].rearrange("p a h t -> p a (h t)")
    onat = sb("onat", [128, TT, D])
    arena = sb("arena", [128, 11 * CH])
    hn = onat
    def tmp(n):
        return arena[:, n * CH:(n + 1) * CH]
    otf = sb("otf", [128, 2, CH])
    rec = sb("rec", [128, 2, CH])
    w5s = otf[:, :, :].rearrange("p a t -> p (a t)")[:, 0:5 * D].rearrange("p (w d) -> p w d", w=5)
    b4s = sb("b4s", [128, 4])
    vbc = sb("vbc", [128, 4, D])
    oT = arena[:, 0:T]
    wos = sb("wos", [128, D])
    rts = sb("rts", [128, E])
    wgs = sb("wgs", [128, E, M])
    wus = sb("wus", [128, E, M])
    wds = sb("wds", [128, E, MC, D])
    identf = sb("identf", [128, 128])
    identb = sb("identb", [128, 128], BF16)
    mask_rows = sb("mask_rows", [128, 128], BF16)
    mask_cols = sb("mask_cols", [128, 128], BF16)
    revi = sb("revi", [128, E], mybir.dt.int32)
    rev = sb("rev", [128, E])
    stats = sb("stats", [128, TT, 6])
    mv = sb("mv", [128, TT, 2])
    rst = sb("rst", [128, 4, TT])
    mpart = sb("mpart", [128, 2, 16, NC])
    mx = sb("mx", [128, 2, 16])
    m3 = sb("m3", [16, 2, 3, 128], BF16)
    mr = sb("mr", [16, 2, 128])
    rden = sb("rden", [128, TPC, HPG, 1])
    gw = rec[:, :, :].rearrange("p a (b t e) -> p (a b) t e", t=TT, e=E)
    gs = sb("gs", [128, 6, TT])
    ps = nc.alloc_psum_tensor("ps", [128, 8, CH], F32)
    pflat = probs[:, :, :, :].rearrange("p a h t -> p (a h t)")
    sgb = [pflat[:, i * CH:i * CH + M] for i in (0, 1)]
    acb = [pflat[:, i * CH:i * CH + M] for i in (2, 3)]
    atb = [pflat[0:MR, i * CH:(i + 1) * CH].rearrange("p (c t) -> p c t", c=MC) for i in (4, 5)]

    split = nc.dram_tensor("split", [2, 3, 128, T], BF16, kind="Internal").ap()

    guard = nc.dram_tensor("guard", [2, 3, 16, 128], BF16, kind="Internal").ap()

    sems = []
    def sem(name):
        s = nc.alloc_semaphore(name)
        sems.append(s)
        return s

    load_s = sem("load_s")
    const_s = sem("const_s")
    dve_s = sem("dve_s")
    pool_s = sem("pool_s")
    var_s = sem("var_s")
    std_s = sem("std_s")
    hn_s = sem("hn_s")
    htp_s = sem("htp_s")
    ht_s = sem("ht_s")
    proj_s = sem("proj_s")
    rope_s = sem("rope_s")
    y_s = sem("y_s")
    y0_s = sem("y0_s")
    r_s = sem("r_s")
    y1_s = sem("y1_s")
    y2_s = sem("y2_s")
    vp_s = sem("vp_s")
    vv_s = sem("vv_s")
    st_s = [sem("st0_s"), sem("st1_s")]
    par_s = sem("par_s")
    zero_s = sem("zero_s")
    ot0_s = sem("ot0_s")
    ld_s = [sem(f"ld{g}_s") for g in range(NG)]
    scores_s = sem("scores_s")
    exp_s = sem("exp_s")
    pv_s = sem("pv_s")
    mm_s = sem("mm_s")
    mfree_s = sem("mfree_s")
    mx_s = sem("mx_s")
    m3_s = sem("m3_s")
    mrow_s = [sem("mrow0_s"), sem("mrow1_s")]
    gd_s = [sem("gd0_s"), sem("gd1_s")]
    otf_s = sem("otf_s")
    rec_s = sem("rec_s")
    otn_s = sem("otn_s")
    dvb_s = sem("dvb_s")
    otp_s = sem("otp_s")
    ot_s = sem("ot_s")
    wo_s = sem("wo_s")
    dvc_s = sem("dvc_s")
    x2_s = sem("x2_s")
    ms_s = sem("ms_s")
    sd2_s = sem("sd2_s")
    h2_s = sem("h2_s")
    h2p_s = sem("h2p_s")
    h2t_s = sem("h2t_s")
    lg_s = sem("lg_s")
    mxl_s = sem("mxl_s")
    ex_s = sem("ex_s")
    gu_s = sem("gu_s")
    sg_s = sem("sg_s")
    ac_s = sem("ac_s")
    tp_s = sem("tp_s")
    at_s = sem("at_s")
    dn_s = sem("dn_s")
    acc_s = sem("acc_s")
    all_sems = range(min(s.num for s in sems), max(s.num for s in sems) + 1)
    assert len(all_sems) == len(sems)

    chunks, events = core_schedule()

    def group_end(g):
        return 2 * sum(TPC * (c + 1) for gg, c in chunks if gg <= g)

    pbuf = arena[:, 8 * CH:11 * CH].bitcast(BF16).rearrange("p (b l t) -> p b l t", b=2, l=3)

    def parts(i):
        return pbuf[:, i % 2, :, :]

    with nc.Block() as block:

        @block.sync
        def _(sp):
            sp.dma_start(xs[:, :, :], x_in.rearrange("(t p) d -> p t d", p=128)).then_inc(load_s, 16)
            sp.dma_start(rts[:, :], router).then_inc(load_s, 16)
            sp.dma_start(wgs[:, :, :], w_gate.rearrange("e d m -> d e m")).then_inc(load_s, 16)
            sp.dma_start(wus[:, :, :], w_up.rearrange("e d m -> d e m")).then_inc(load_s, 16)
            sp.dma_start(wds[0:MR, :, :, :], w_down.rearrange("e (c p) d -> p e c d", p=MR)).then_inc(load_s, 16)
            sp.wait_ge(load_s, 80)

        @block.gpsimd
        def _(pool):
            n = 0
            for tile, value in ((identf, 0.0), (identb, 0.0), (mask_rows, 0.0), (mask_cols, 0.0)):
                pool.memset(tile[:, :], value).then_inc(pool_s, 1)
                n += 1
            pool.iota(revi[:, :], pattern=[[-1, E]], base=E, channel_multiplier=0).then_inc(pool_s, 1)
            pool.wait_ge(pool_s, n + 1)
            for tile in (identf, identb):
                pool.affine_select(out=tile[:, :], in_=tile[:, :], compare_op=ALU.not_equal, fill=1.0,
                                   base=0, pattern=[[-1, 128]], channel_multiplier=1).then_inc(const_s, 1)
            pool.affine_select(out=mask_rows[:, :], in_=mask_rows[:, :], compare_op=ALU.is_ge, fill=MASKED,
                               base=0, pattern=[[-1, 128]], channel_multiplier=1).then_inc(const_s, 1)
            pool.affine_select(out=mask_cols[:, :], in_=mask_cols[:, :], compare_op=ALU.is_ge, fill=MASKED,
                               base=0, pattern=[[1, 128]], channel_multiplier=-1).then_inc(const_s, 1)
            pool.tensor_copy(rev[:, :], revi[:, :]).then_inc(const_s, 1)
            pool.wait_ge(const_s, 5)

        @block.vector
        def _(dve):
            dve.memset(vv[:, :, :, :], 1.0).then_inc(dve_s, 1)
            dve.memset(ka[64:96, :, :, :], 1.0).then_inc(dve_s, 1)
            dve.wait_ge(dve_s, 2)

    nc.all_engine_barrier(sems_to_clear=all_sems)

    with nc.Fori(0, NLAYER) as layer:
        with nc.Block() as block:

            @block.sync
            def _(sp):
                one = bass.ds(layer, 1)
                sp.dma_start(w5s[:, :, :], w5[one].rearrange("o p w d -> (o p) w d")).then_inc(par_s, 16)
                sp.dma_start(b4s[:, :], b4[one].rearrange("o p w -> (o p) w")).then_inc(par_s, 16)
                sp.dma_start(vbc[:, :, :].rearrange("p v d -> p (v d)"),
                             vecs[one].broadcast_to([128, 4 * D])).then_inc(par_s, 16)
                sp.dma_start(wos[:, :], wo_w[one].rearrange("o p d -> (o p) d")).then_inc(par_s, 16)
                sp.dma_start(rtab, rope[one].rearrange("o p a t -> (o p) a t")).then_inc(par_s, 16)
                for i in range(2 * NC):
                    c, which = i // 2, i % 2
                    sp.wait_ge(y2_s, i + 1)
                    sp.dma_start(split[which, :, :, c * CH:(c + 1) * CH].rearrange("l p t -> p l t"),
                                 parts(i)).then_inc(st_s[i % 2], 16)
                for k in (0, 1):
                    sp.wait_ge(st_s[k], 16 * NC)

            @block.vector
            def _(dve):
                n = [0]

                def link(ins):
                    n[0] += 1
                    ins.then_inc(dve_s, 1)
                    dve.wait_ge(dve_s, n[0])

                for t in range(TT):
                    ins = dve.bn_stats(stats[:, t, :], xs[:, t, :])
                link(ins)
                for t in range(TT):
                    ins = dve.bn_aggr(mv[:, t, :], stats[:, t, :])
                link(ins)
                dve.tensor_scalar(rst[:, 0, :], mv[:, :, 1], LN_EPS, None, ALU.add).then_inc(var_s, 1)
                dve.wait_ge(std_s, 1)
                link(dve.reciprocal(rst[:, 1, :], rst[:, 0, :]))
                for t in range(TT):
                    ins = dve.tensor_scalar(x1[:, t, :], xs[:, t, :], mv[:, t, 0:1], rst[:, 1, t:t + 1],
                                            ALU.subtract, ALU.mult)
                link(ins)
                for t in range(TT):
                    ins = dve.tensor_tensor_reduce(hn[:, t, :], x1[:, t, :], x1[:, t, :], 1.0, 0.0,
                                                   ALU.mult, ALU.add, rst[:, 2, t:t + 1])
                link(ins)
                dve.tensor_scalar(rst[:, 2, :], rst[:, 2, :], 1.0 / D, RMS_EPS, ALU.mult, ALU.add).then_inc(var_s, 1)
                dve.wait_ge(std_s, 2)
                link(dve.reciprocal(rst[:, 3, :], rst[:, 2, :]))
                with dve.If(layer == 1):
                    dve.memset(rst[:, 0, :], 1.0).then_inc(dve_s, 1)
                with dve.If(layer != 1):
                    dve.tensor_copy(rst[:, 0, :], rst[:, 3, :]).then_inc(dve_s, 1)
                n[0] += 1
                dve.wait_ge(dve_s, n[0])
                dve.wait_ge(par_s, 80)
                for t in range(TT):
                    dve.scalar_tensor_tensor(hn[:, t, :], x1[:, t, :], rst[:, 0, t:t + 1], vbc[:, V_LN1, :],
                                             ALU.mult, ALU.mult).then_inc(hn_s, 1)

                def remainder(i):
                    dve.wait_ge(y0_s, i + 1)
                    dve.tensor_tensor(tmp(6 + i % 2), tmp(4 + i % 2), parts(i)[:, 0, :], ALU.subtract).then_inc(r_s, 1)

                for c in range(NC):
                    cols = slice(c * CH, (c + 1) * CH)
                    for which in (0, 1):
                        i = 2 * c + which
                        if i >= 2:
                            dve.wait_ge(y_s, i - 1)
                        for k in (0, 1):
                            dve.wait_ge(proj_s, 2 * i + k + 1)
                            dve.scalar_tensor_tensor(tmp(2 * (i % 2) + k), ps[:, 2 + 2 * which + k, :],
                                                     b4s[:, 2 * which + k:2 * which + k + 1], rtab[:, k, cols],
                                                     ALU.add, ALU.mult).then_inc(rope_s, 1)
                        if i:
                            if i >= 3:
                                dve.wait_ge(y2_s, i - 2)
                            remainder(i - 1)
                    dve.wait_ge(vp_s, c + 1)
                    dve.tensor_tensor(vv[:, TPC * c:TPC * (c + 1), :, 0:HD],
                                      ps[:, 6 + c % 2, :].rearrange("p (t h d) -> p t h d", t=TPC, h=H),
                                      vbc[:, V_BV:V_BV + 1, :].rearrange("p o (h d) -> p o h d", h=H).broadcast_to(
                                          [128, TPC, H, HD]), ALU.add).then_inc(vv_s, 1)
                dve.wait_ge(y2_s, 2 * NC - 2)
                remainder(2 * NC - 1)

            @block.gpsimd
            def _(pool):
                def third(i):
                    pool.wait_ge(y1_s, i + 1)
                    pool.tensor_tensor(parts(i)[:, 2, :], tmp(6 + i % 2), parts(i)[:, 1, :],
                                       ALU.subtract).then_inc(y2_s, 1)

                for i in range(2 * NC):
                    pool.wait_ge(rope_s, 2 * i + 2)
                    if i >= 2:
                        pool.wait_ge(r_s, i - 1)
                    pool.tensor_tensor(tmp(4 + i % 2), tmp(2 * (i % 2)), tmp(2 * (i % 2) + 1),
                                       ALU.add).then_inc(y_s, 1)
                    if i:
                        third(i - 1)
                third(2 * NC - 1)

            @block.scalar
            def _(act):
                act.wait_ge(var_s, 1)
                act.activation(rst[:, 0, :], rst[:, 0, :], ACT.Sqrt).then_inc(std_s, 1)
                act.wait_ge(var_s, 2)
                act.activation(rst[:, 2, :], rst[:, 2, :], ACT.Sqrt).then_inc(std_s, 1)

                def second(i):
                    act.wait_ge(r_s, i + 1)
                    act.activation(parts(i)[:, 1, :], tmp(6 + i % 2), ACT.Copy).then_inc(y1_s, 1)

                for c in range(NC):
                    act.wait_ge(htp_s, c + 1)
                    act.activation(hT[:, c * CH:(c + 1) * CH], ps[:, c % 2, :], ACT.Copy).then_inc(ht_s, 1)
                    for i in (2 * c, 2 * c + 1):
                        act.wait_ge(y_s, i + 1)
                        if i >= 2:
                            act.wait_ge(st_s[i % 2], 16 * (i // 2))
                        act.activation(parts(i)[:, 0, :], tmp(4 + i % 2), ACT.Copy).then_inc(y0_s, 1)
                        if i:
                            second(i - 1)
                second(2 * NC - 1)

            @block.tensor
            def _(pe):
                for c in range(NC):
                    for k in range(TPC):
                        t = TPC * c + k
                        pe.wait_ge(hn_s, t + 1)
                        if c >= 2:
                            pe.wait_ge(ht_s, c - 1)
                        ins = pe.transpose(ps[:, c % 2, k * 128:(k + 1) * 128], hn[:, t, :], identf[:, :])
                    ins.then_inc(htp_s, 1)
                    pe.wait_ge(ht_s, c + 1)
                    pe.wait_ge(par_s, 80)
                    for w in range(4):
                        if c:
                            pe.wait_ge(rope_s, 4 * (c - 1) + w + 1)
                        pe.matmul(ps[:, 2 + w, :], w5s[:, w, :], hT[:, c * CH:(c + 1) * CH],
                                  start=True, stop=True).then_inc(proj_s, 1)
                    if c >= 2:
                        pe.wait_ge(vv_s, c - 1)
                    for k in range(TPC):
                        t = TPC * c + k
                        ins = pe.matmul(ps[:, 6 + c % 2, k * 128:(k + 1) * 128], hT[:, t * 128:(t + 1) * 128],
                                        w5s[:, W_V, :], start=True, stop=True)
                    ins.then_inc(vp_s, 1)

        with nc.Block() as block:

            @block.sync
            def _(sp):
                def load(g):
                    b = g % 2
                    sp.wait_ge(zero_s, g + 1)
                    if g >= 2:
                        sp.wait_ge(scores_s, group_end(g - 2))
                    for s in range(9):
                        for which, level, dst in ((0, s % 3, qa), (1, s // 3, ka)):
                            src = split[which, level, g * HPG * HD:(g + 1) * HPG * HD, :]
                            sp.dma_start(dst[s * HD:(s + 1) * HD, b, :, :],
                                         src.rearrange("(h i) t -> i h t", i=HD)).then_inc(ld_s[g], 16)

                load(0)
                load(1)
                for ev in events:
                    if ev[0] == "maxout":
                        j = ev[1]
                        g, c = chunks[j]
                        sp.wait_ge(m3_s, j + 1)
                        if j >= 2:
                            sp.wait_ge(mrow_s[j % 2], 16 * (j // 2))
                        sp.dma_start(guard[j % 2].rearrange("l r t -> r l t"), m3[:, j % 2, :, :]).then_inc(gd_s[j % 2], 16)
                        sp.wait_ge(gd_s[j % 2], 16 * (j // 2 + 1))
                        sp.dma_start(qa[GUARD:GUARD + 3, g % 2, :, c * CH:(c + 1) * CH],
                                     guard[j % 2].rearrange("l (h q) t -> l h (q t)", h=HPG)).then_inc(mrow_s[j % 2], 16)
                    elif ev[0] == "reload" and ev[1] + 2 < NG:
                        load(ev[1] + 2)

            @block.tensor
            def _(pe):
                mi = 0
                pe.wait_ge(ot0_s, 1)
                for ev in events:
                    kind = ev[0]
                    if kind in ("rowmax", "maxout", "normalise"):
                        bank = 4 + mi % 2
                        if mi >= 2:
                            pe.wait_ge(mfree_s, mi - 1)
                        mi += 1
                    if kind == "rowmax":
                        _, j, qt, h, kc = ev
                        g, c = chunks[j]
                        b = g % 2
                        if qt == 0 and h == 0 and kc == 0:
                            pe.wait_ge(ld_s[g], 16 * 18)
                        tile = TPC * c + qt
                        n = min(CH, (tile + 1) * 128 - kc * CH)
                        diag = kc == c
                        ins = pe.matmul(ps[:, bank, 0:n], qa[0:KROWS, b, h, tile * 128:(tile + 1) * 128],
                                        ka[0:KROWS, b, h, kc * CH:kc * CH + n], start=True, stop=not diag)
                        if diag:
                            ins = pe.matmul(ps[:, bank, n - 128:n], identb[:, :], mask_rows[:, :],
                                            start=False, stop=True)
                        ins.then_inc(mm_s, 1)
                    elif kind == "maxout":
                        j = ev[1]
                        pe.wait_ge(mx_s, j + 1)
                        pe.transpose(ps[0:16, bank, 0:128], mx[:, j % 2, :], identf[:, :]).then_inc(mm_s, 1)
                    elif kind == "normalise":
                        j = ev[1]
                        pe.wait_ge(otf_s, j + 1)
                        for k in range(TPC):
                            ins = pe.transpose(ps[:, bank, k * 128:(k + 1) * 128],
                                               otf[:, j % 2, k * 128:(k + 1) * 128], identf[:, :])
                        ins.then_inc(mm_s, 1)
                    elif kind == "scores":
                        _, s, j, kt, pair = ev
                        g, c = chunks[j]
                        b = g % 2
                        if kt == 0 and pair == 0:
                            pe.wait_ge(mrow_s[j % 2], 16 * (j // 2 + 1))
                        q0 = max(0, kt - TPC * c) * 128
                        n = CH - q0
                        diag = kt >= TPC * c
                        u = 2 * s + pair
                        if u >= 2:
                            pe.wait_ge(exp_s, u - 1)
                        for k in (0, 1):
                            h = 2 * pair + k
                            dst = ps[:, 2 * (u % 2) + k, 0:n]
                            ins = pe.matmul(dst, ka[0:KROWS, b, h, kt * 128:(kt + 1) * 128],
                                            qa[0:KROWS, b, h, c * CH + q0:(c + 1) * CH],
                                            start=True, stop=not diag)
                            if diag:
                                ins = pe.matmul(dst[:, 0:128], identb[:, :], mask_cols[:, :],
                                                start=False, stop=True)
                        ins.then_inc(scores_s, 1)
                    elif kind == "values":
                        _, s, j, kt = ev
                        g, c = chunks[j]
                        q0 = max(0, kt - TPC * c) * 128
                        pe.wait_ge(exp_s, 2 * s + 2)
                        if kt == 0 and j >= 2:
                            pe.wait_ge(otf_s, j - 1)
                        for h in range(HPG):
                            ins = pe.matmul(ps[32 * h:32 * h + HD + 1, 6 + j % 2, q0:CH],
                                            vv[:, kt, g * HPG + h, :], probs[:, s % 2, h, 0:CH - q0],
                                            start=kt == 0, stop=kt == TPC * (c + 1) - 1)
                        ins.then_inc(pv_s, 1)

            @block.scalar
            def _(act):
                for ev in events:
                    if ev[0] == "scores":
                        _, s, j, kt, pair = ev
                        g, c = chunks[j]
                        n = CH - max(0, kt - TPC * c) * 128
                        u = 2 * s + pair
                        if s >= 2 and pair == 0:
                            act.wait_ge(pv_s, s - 1)
                        act.wait_ge(scores_s, u + 1)
                        act.activation(probs[:, s % 2, 2 * pair:2 * pair + 2, 0:n],
                                       ps[:, 2 * (u % 2):2 * (u % 2) + 2, 0:n], ACT.Exp,
                                       scale=SCALE).then_inc(exp_s, 1)
                    elif ev[0] == "evacuate":
                        j = ev[1]
                        act.wait_ge(pv_s, sum(TPC * (c + 1) for _, c in chunks[:j + 1]))
                        if j >= 2:
                            act.wait_ge(otn_s, j - 1)
                        act.activation(otf[:, j % 2, :], ps[:, 6 + j % 2, :], ACT.Copy).then_inc(otf_s, 1)

            @block.vector
            def _(dve):
                dve.memset(ps[:, 6:8, :], 0.0).then_inc(ot0_s, 1)
                mi = 0
                n = [0]

                def link(ins):
                    n[0] += 1
                    ins.then_inc(dvb_s, 1)
                    dve.wait_ge(dvb_s, n[0])

                for ev in events:
                    kind = ev[0]
                    if kind in ("rowmax", "maxout", "normalise"):
                        bank = 4 + mi % 2
                        mi += 1
                        dve.wait_ge(mm_s, mi)
                    if kind == "rowmax":
                        _, j, qt, h, kc = ev
                        g, c = chunks[j]
                        w = min(CH, (TPC * c + qt + 1) * 128 - kc * CH)
                        dve.tensor_reduce(mpart[:, j % 2, 4 * h + qt, kc:kc + 1], ps[:, bank, 0:w],
                                          axis=AX.X, op=ALU.max).then_inc(mfree_s, 1)
                        if qt == TPC - 1 and h == HPG - 1 and kc == c:
                            dve.wait_ge(mfree_s, mi)
                            if j >= 2:
                                dve.wait_ge(m3_s, j - 1)
                            dve.tensor_reduce(mx[:, j % 2, :], mpart[:, j % 2, :, 0:c + 1], axis=AX.X,
                                              op=ALU.max, negate=True).then_inc(mx_s, 1)
                    elif kind == "maxout":
                        j = ev[1]
                        if j >= 2:
                            dve.wait_ge(mrow_s[j % 2], 16 * (j // 2))
                        src = ps[0:16, bank, 0:128]
                        link(dve.tensor_copy(m3[:, j % 2, 0, :], src))
                        dve.tensor_tensor(mr[:, 0, :], src, m3[:, j % 2, 0, :], ALU.subtract).then_inc(mfree_s, 1)
                        dve.wait_ge(mfree_s, mi)
                        link(dve.tensor_copy(m3[:, j % 2, 1, :], mr[:, 0, :]))
                        dve.tensor_tensor(m3[:, j % 2, 2, :], mr[:, 0, :], m3[:, j % 2, 1, :],
                                          ALU.subtract).then_inc(m3_s, 1)
                    elif kind == "normalise":
                        j = ev[1]
                        g, c = chunks[j]
                        turned = ps[:, bank, :].rearrange("p (q h r) -> p q h r", q=TPC, r=32)
                        link(dve.reciprocal(rden[:, :, :, :], turned[:, :, :, HD:HD + 1]))
                        dve.tensor_tensor(
                            onat[:, TPC * c:TPC * (c + 1), 32 * g:32 * g + 32].rearrange("p q (h i) -> p q h i", i=HD),
                            turned[:, :, :, 0:HD], rden[:, :, :, :].broadcast_to([128, TPC, HPG, HD]),
                            ALU.mult).then_inc(mfree_s, 1)
                        dve.wait_ge(mfree_s, mi)
                        dve.engine_nop().then_inc(otn_s, 1)

            @block.gpsimd
            def _(pool):
                zeros = lambda b: qa[64:96, b, :, :].rearrange("p h t -> p (h t)").bitcast(F32)
                pool.memset(zeros(0), 0.0).then_inc(zero_s, 1)
                pool.memset(zeros(1), 0.0).then_inc(zero_s, 1)
                pool.wait_ge(zero_s, 2)
                for ev in events:
                    if ev[0] == "reload" and ev[1] + 2 < NG:
                        pool.wait_ge(scores_s, group_end(ev[1]))
                        pool.memset(zeros(ev[1] % 2), 0.0).then_inc(zero_s, 1)
                        pool.wait_ge(zero_s, ev[1] + 3)

        with nc.Block() as block:

            @block.tensor
            def _(pe):
                def project(c):
                    pe.wait_ge(ot_s, c + 1)
                    if c >= 2:
                        pe.wait_ge(x2_s, c - 1)
                    for k in range(TPC):
                        t = TPC * c + k
                        ins = pe.matmul(ps[:, 2 + c % 2, k * 128:(k + 1) * 128], oT[:, t * 128:(t + 1) * 128],
                                        wos[:, :], start=True, stop=True)
                    ins.then_inc(wo_s, 1)

                for c in range(NC):
                    if c >= 2:
                        pe.wait_ge(ot_s, c - 1)
                    for k in range(TPC):
                        ins = pe.transpose(ps[:, c % 2, k * 128:(k + 1) * 128], onat[:, TPC * c + k, :], identf[:, :])
                    ins.then_inc(otp_s, 1)
                    if c:
                        project(c - 1)
                project(NC - 1)
                for c in range(NC):
                    if c >= 2:
                        pe.wait_ge(h2t_s, c - 1)
                    for k in range(TPC):
                        t = TPC * c + k
                        pe.wait_ge(h2_s, t + 1)
                        ins = pe.transpose(ps[:, 4 + c % 2, k * 128:(k + 1) * 128], hn[:, t, :], identf[:, :])
                    ins.then_inc(h2p_s, 1)
                for t in range(TT):
                    pe.wait_ge(h2t_s, t // TPC + 1)
                    ins = pe.matmul(ps[:, 6, t * E:(t + 1) * E], hT[:, t * 128:(t + 1) * 128], rts[:, :],
                                    start=True, stop=True)
                ins.then_inc(lg_s, 1)

            @block.scalar
            def _(act):
                for c in range(NC):
                    act.wait_ge(otp_s, c + 1)
                    act.activation(oT[:, c * CH:(c + 1) * CH], ps[:, c % 2, :], ACT.Copy).then_inc(ot_s, 1)
                act.wait_ge(ms_s, 1)
                act.activation(rst[:, 2, :], rst[:, 2, :], ACT.Sqrt).then_inc(sd2_s, 1)
                for c in range(NC):
                    act.wait_ge(h2p_s, c + 1)
                    act.activation(hT[:, c * CH:(c + 1) * CH], ps[:, 4 + c % 2, :], ACT.Copy).then_inc(h2t_s, 1)
                act.wait_ge(mxl_s, 1)
                act.activation(gw[:, 0, :, :], gw[:, 0, :, :], ACT.Exp).then_inc(ex_s, 1)

            @block.vector
            def _(dve):
                n = [0]

                def link(ins):
                    n[0] += 1
                    ins.then_inc(dvc_s, 1)
                    dve.wait_ge(dvc_s, n[0])

                for c in range(NC):
                    dve.wait_ge(wo_s, c + 1)
                    rows = slice(TPC * c, TPC * (c + 1))
                    link(dve.tensor_tensor(rec[:, 0, :].rearrange("p (t d) -> p t d", d=D),
                                           ps[:, 2 + c % 2, :].rearrange("p (t d) -> p t d", d=D),
                                           vbc[:, V_BO:V_BO + 1, :].broadcast_to([128, TPC, D]), ALU.add))
                    y = rec[:, 0, :].rearrange("p (t d) -> p t d", d=D)
                    with dve.If(layer == 1):
                        dve.tensor_tensor(xs[:, rows, :], xs[:, rows, :], y, ALU.add).then_inc(x2_s, 1)
                    with dve.If(layer != 1):
                        dve.tensor_tensor(x1[:, rows, :], x1[:, rows, :], y, ALU.add).then_inc(x2_s, 1)
                    dve.wait_ge(x2_s, c + 1)
                for t in range(TT):
                    ins = dve.tensor_tensor_reduce(hn[:, t, :], x1[:, t, :], x1[:, t, :], 1.0, 0.0,
                                                   ALU.mult, ALU.add, rst[:, 2, t:t + 1])
                link(ins)
                dve.tensor_scalar(rst[:, 2, :], rst[:, 2, :], 1.0 / D, RMS_EPS, ALU.mult, ALU.add).then_inc(ms_s, 1)
                dve.wait_ge(sd2_s, 1)
                link(dve.reciprocal(rst[:, 3, :], rst[:, 2, :]))
                for t in range(TT):
                    dve.scalar_tensor_tensor(hn[:, t, :], x1[:, t, :], rst[:, 3, t:t + 1], vbc[:, V_LN2, :],
                                             ALU.mult, ALU.mult).then_inc(h2_s, 1)
                dve.wait_ge(lg_s, 1)
                lg = ps[:, 6, 0:TT * E].rearrange("p (t e) -> p t e", e=E)
                shape = [128, TT, E]

                def wide(k):
                    return gs[:, k, :].rearrange("p (t o) -> p t o", o=1).broadcast_to(shape)

                revb = rev[:, :].rearrange("p (o e) -> p o e", o=1).broadcast_to(shape)
                link(dve.tensor_reduce(gs[:, 0, :], lg, axis=AX.X, op=ALU.max))
                dve.tensor_tensor(gw[:, 0, :, :], lg, wide(0), ALU.subtract).then_inc(mxl_s, 1)
                dve.wait_ge(ex_s, 1)
                link(dve.tensor_reduce(gs[:, 1, :], gw[:, 0, :, :], axis=AX.X, op=ALU.add))
                link(dve.reciprocal(gs[:, 0, :], gs[:, 1, :]))
                link(dve.tensor_tensor(gw[:, 1, :, :], gw[:, 0, :, :], wide(0), ALU.mult))
                def pick(src, dst, peak, at):
                    link(dve.tensor_reduce(gs[:, peak, :], src, axis=AX.X, op=ALU.max))
                    link(dve.tensor_tensor(gw[:, 7, :, :], src, wide(peak), ALU.is_equal))
                    link(dve.tensor_tensor(gw[:, 7, :, :], gw[:, 7, :, :], revb, ALU.mult))
                    link(dve.tensor_reduce(gs[:, at, :], gw[:, 7, :, :], axis=AX.X, op=ALU.max))
                    link(dve.tensor_tensor(dst, revb, wide(at), ALU.is_equal))

                pick(gw[:, 1, :, :], gw[:, 2, :, :], 2, 3)
                link(dve.scalar_tensor_tensor(gw[:, 3, :, :], gw[:, 2, :, :], -2.0, gw[:, 1, :, :], ALU.mult, ALU.add))
                pick(gw[:, 3, :, :], gw[:, 4, :, :], 4, 3)
                link(dve.tensor_tensor(gs[:, 5, :], gs[:, 2, :], gs[:, 4, :], ALU.add))
                link(dve.reciprocal(gs[:, 0, :], gs[:, 5, :]))
                link(dve.tensor_tensor(gw[:, 5, :, :], gw[:, 2, :, :], gw[:, 4, :, :], ALU.add))
                link(dve.tensor_tensor(gw[:, 5, :, :], gw[:, 5, :, :], gw[:, 1, :, :], ALU.mult))
                link(dve.tensor_tensor(gw[:, 6, :, :], gw[:, 5, :, :], wide(0), ALU.mult))

        NU = E * TT
        with nc.Block() as block:

            @block.tensor
            def _(pe):
                with pe.If(layer != 1):
                    for i in range(NU + 2):
                        if i < NU:
                            e, t = divmod(i, TT)
                            if i >= 2:
                                pe.wait_ge(ac_s, i - 1)
                            for k, w in ((0, wgs), (1, wus)):
                                ins = pe.matmul(ps[:, 2 * (i % 2) + k, 0:M], hT[:, t * 128:(t + 1) * 128],
                                                w[:, e, :], start=True, stop=True)
                                ins.then_inc(gu_s, 1)
                        if 1 <= i <= NU:
                            u = i - 1
                            pe.wait_ge(ac_s, u + 1)
                            if u >= 2:
                                pe.wait_ge(at_s, u - 1)
                            for k in range(MC):
                                ins = pe.transpose(ps[0:MR, 4 + u % 2, k * 128:(k + 1) * 128],
                                                   acb[u % 2][:, k * MR:(k + 1) * MR], identf[:, :])
                            ins.then_inc(tp_s, 1)
                        if i >= 2:
                            u = i - 2
                            e = u // TT
                            pe.wait_ge(at_s, u + 1)
                            if u >= 2:
                                pe.wait_ge(acc_s, u - 1)
                            for k in range(MC):
                                ins = pe.matmul(ps[:, 6 + u % 2, 0:D], atb[u % 2][:, k, :], wds[0:MR, e, k, :],
                                                start=k == 0, stop=k == MC - 1)
                            ins.then_inc(dn_s, 1)

            @block.scalar
            def _(act):
                with act.If(layer != 1):
                    for i in range(NU + 1):
                        if i < NU:
                            act.wait_ge(gu_s, 2 * i + 1)
                            if i >= 2:
                                act.wait_ge(ac_s, i - 1)
                            act.activation(sgb[i % 2], ps[:, 2 * (i % 2), 0:M], ACT.Silu).then_inc(sg_s, 1)
                        if i:
                            u = i - 1
                            act.wait_ge(tp_s, u + 1)
                            if u >= 2:
                                act.wait_ge(dn_s, u - 1)
                            act.activation(atb[u % 2], ps[0:MR, 4 + u % 2, :].rearrange("p (c t) -> p c t", c=MC),
                                           ACT.Copy).then_inc(at_s, 1)

            @block.vector
            def _(dve):
                with dve.If(layer != 1):
                    for i in range(NU + 2):
                        if i < NU:
                            dve.wait_ge(sg_s, i + 1)
                            dve.wait_ge(gu_s, 2 * i + 2)
                            if i >= 2:
                                dve.wait_ge(tp_s, i - 1)
                            dve.tensor_tensor(acb[i % 2], sgb[i % 2], ps[:, 2 * (i % 2) + 1, 0:M],
                                              ALU.mult).then_inc(ac_s, 1)
                        if i >= 2:
                            u = i - 2
                            e, t = divmod(u, TT)
                            dve.wait_ge(dn_s, u + 1)
                            if u >= TT:
                                dve.wait_ge(acc_s, u - TT + 1)
                            dve.scalar_tensor_tensor(x1[:, t, :], ps[:, 6 + u % 2, 0:D], gw[:, 6, t, e:e + 1],
                                                     x1[:, t, :], ALU.mult, ALU.add).then_inc(acc_s, 1)
                    dve.wait_ge(acc_s, NU)
                    dve.scalar_tensor_tensor(xs[:, :, :].rearrange("p t d -> p (t d)"),
                                             x1[:, :, :].rearrange("p t d -> p (t d)"), 0.5,
                                             xs[:, :, :].rearrange("p t d -> p (t d)"),
                                             ALU.mult, ALU.add).then_inc(acc_s, 1)

        nc.all_engine_barrier(sems_to_clear=all_sems)

    with nc.Block() as block:

        @block.sync
        def _(sp):
            sp.dma_start(out.rearrange("(t p) d -> p t d", p=128), xs[:, :, :]).then_inc(load_s, 16)
            sp.wait_ge(load_s, 16)


def rotary_tables():
    i = np.arange(HD // 2, dtype=np.float32)
    pos = np.arange(T, dtype=np.float32)
    ffn = pos[:, None] * (np.float32(1.0) / np.float32(10000.0) ** (2 * i / np.float32(HD)))[None, :]
    att = pos[:, None] * (np.float32(10000.0) ** (np.float32(-2.0) * i / np.float32(HD)))[None, :]
    tabs = []
    for angle, sign in ((ffn, -1.0), (att, 1.0), (ffn, -1.0)):
        angle = angle.astype(np.float32)
        cos, sin = np.cos(angle), np.sin(angle)
        c8 = np.concatenate([cos, cos], 1).T
        s8 = np.concatenate([np.float32(sign) * sin, sin], 1).T
        tabs.append(np.stack([np.tile(c8, (H, 1)), np.tile(s8, (H, 1))], 1))
    return np.ascontiguousarray(np.stack(tabs).astype(np.float32))


def kernel(**inputs):
    import concourse.bacc as bacc
    from concourse.bass_utils import run_bass_kernel_spmd as run

    v = {k: np.asarray(a) for k, a in inputs.items()}
    f = "L0_ffn_"
    a = "L0_attn_"
    other_half = np.arange(H * HD).reshape(H, 2, HD // 2)[:, ::-1, :].reshape(-1)
    rep = H // (v[f + "wk"].shape[1] // HD)

    def heads(w):
        return np.repeat(w.reshape(D, -1, HD), rep, axis=1).reshape(D, H * HD)

    fq, fk, fv = v[f + "wq"], heads(v[f + "wk"]), heads(v[f + "wv"])
    ffn5 = np.stack([fq, fq[:, other_half], fk, fk[:, other_half], fv], 1)
    aq, ak, av = v[a + "Wq"].T, v[a + "Wk"].T, v[a + "Wv"].T
    att5 = np.stack([aq, aq, ak, ak, av], 1)
    zero, one = np.zeros(D, np.float32), np.ones(D, np.float32)
    b_ffn = np.stack([zero] * 4, 1)
    b_att = np.stack([v[a + "bq"], v[a + "bq"], v[a + "bk"], v[a + "bk"]], 1)
    v_ffn = np.concatenate([v[f + "ln1_w"], zero, zero, v[f + "ln2_w"]])
    v_att = np.concatenate([one, v[a + "bv"], v[a + "bo"], one])

    wo_f, wo_a = v[f + "wo"], v[a + "Wo"].T
    arrays = {
        "x_in": v[a + "x"].reshape(T, D),
        "w5": np.stack([ffn5, att5, ffn5]),
        "b4": np.stack([b_ffn, b_att, b_ffn]),
        "vecs": np.stack([v_ffn, v_att, v_ffn]),
        "wo_w": np.stack([wo_f, wo_a, wo_f]),
        "rope": rotary_tables(),
        "router": v[f + "router_w"],
        "w_gate": v[f + "w_gate"],
        "w_up": v[f + "w_up"],
        "w_down": v[f + "w_down"],
    }
    arrays = {k: np.ascontiguousarray(b) for k, b in arrays.items()}
    nc = bacc.Bacc("TRN2", target_bir_lowering=False, num_devices=1)
    args = [nc.dram_tensor(k, b.shape, mybir.dt.from_np(b.dtype), kind="ExternalInput").ap() for k, b in arrays.items()]
    out = nc.dram_tensor("out", (T, D), F32, kind="ExternalOutput").ap()
    macaron_kernel(nc, *args, out)
    r = run(nc, [arrays], core_ids=[0])
    return r.results[0]["out"].reshape(1, T, D)
```

```python
import numpy as np
import concourse.bass as bass
from concourse import mybir

F32 = mybir.dt.float32
BF16 = mybir.dt.bfloat16
I32 = mybir.dt.int32
ALU = mybir.AluOpType
ACT = mybir.ActivationFunctionType
AX = mybir.AxisListType

T, D = 2048, 128
TT = T // 128
H, HD = 16, 8
HPG = 4
NG = H // HPG
CH = 512
NC = T // CH
TPC = CH // 128
KROWS = 96
GUARD = 9 * HD
E, M = 8, 448
MC, MR = 4, 112
NLAYER = 3
SCALE = float(1.0 / np.sqrt(np.float32(HD)))
MASKED = -1e30
LN_EPS, RMS_EPS = 1e-5, 1e-6
W_Q, W_QR, W_K, W_KR, W_V = range(5)
V_LN1, V_BV, V_BO, V_LN2 = range(4)
TOPK = 2
NSLOT = (TOPK * T + E * 127) // 128
ROW = D + 2
XR, OR = 8, 4


def core_schedule():
    chunks = []
    for g in range(NG):
        cs = list(range(NC))
        chunks += [(g, c) for c in (cs if g % 2 == 0 else cs[::-1])]
    maxima, due = [], []
    for j, (g, c) in enumerate(chunks):
        units = [("rowmax", j, qt, h, kc) for qt in range(TPC) for h in range(HPG) for kc in range(c + 1)]
        if j:
            units.insert(2, ("maxout", j - 1))
        maxima += units
        due.append(len(maxima))
    maxima.append(("maxout", len(chunks) - 1))
    due = [min(d + 3, len(maxima)) for d in due]
    steps = [(j, kt) for j, (g, c) in enumerate(chunks) for kt in range(TPC * (c + 1))]
    total = len(steps)
    events, done = [], 0
    start_of = {}
    for s, (j, kt) in enumerate(steps):
        start_of.setdefault(j, s)
    need = [0] * (total + 1)
    ahead = 5
    for j in range(len(chunks)):
        need[max(0, start_of[j] - (ahead if j else 0))] = max(due[j], need[max(0, start_of[j] - ahead)])
    want = [0] * total
    level = 0.0
    for s in range(total):
        rate = 0.0
        if need[s] > level:
            level = need[s]
        for j in range(len(chunks)):
            at = start_of[j] - ahead
            if at > s and due[j] > level:
                rate = max(rate, (due[j] - level) / (at - s))
        want[s] = int(np.ceil(level))
        level = min(len(maxima), level + rate)
    for s, (j, kt) in enumerate(steps):
        todo = max(0, min(want[s], len(maxima)) - done)
        gap = []
        for slot in range(4):
            k = (todo + 3 - slot) // 4
            gap.append(maxima[done:done + k])
            done += k
        if s == 0:
            for k in range(4):
                events += gap[k]
                gap[k] = []
        events.append(("scores", s, j, kt, 0))
        events += gap[0]
        events.append(("scores", s, j, kt, 1))
        events += gap[1]
        if s:
            pj, pk = steps[s - 1]
            events.append(("values", s - 1, pj, pk))
            if pj != j:
                events.append(("evacuate", pj))
        events += gap[2]
        if j and kt == 2:
            events.append(("normalise", j - 1))
        events += gap[3]
        if kt == TPC * (chunks[j][1] + 1) - 1 and chunks[j][1] == (NC - 1 if chunks[j][0] % 2 == 0 else 0):
            events.append(("reload", chunks[j][0]))
    while done < len(maxima):
        events.append(maxima[done])
        done += 1
    j = len(chunks) - 1
    events.append(("values", total - 1, j, steps[-1][1]))
    events.append(("evacuate", j))
    events.append(("normalise", j))
    return chunks, events


def macaron_kernel(nc, x_in, w5, b4, vecs, wo_w, rope, router, w_gate, w_up, w_down, out):
    def sb(name, shape, dt=F32):
        return nc.alloc_sbuf_tensor(name, shape, dt)

    xs = sb("xs", [128, TT, D])
    x1 = sb("x1", [128, TT, D])
    hT = sb("hT", [128, T])
    qa = sb("qa", [128, 2, HPG, T], BF16)
    ka = sb("ka", [128, 2, HPG, T], BF16)
    vv = sb("vv", [128, TT, H, HD + 1])
    probs = sb("probs", [128, 2, HPG, CH])
    rtab = probs[:, :, :, :].rearrange("p a h t -> p a (h t)")
    onat = sb("onat", [128, TT, D])
    arena = sb("arena", [128, 11 * CH])
    hn = onat
    def tmp(n):
        return arena[:, n * CH:(n + 1) * CH]
    otf = sb("otf", [128, 2, CH])
    rec = sb("rec", [128, 2, CH])
    w5s = otf[:, :, :].rearrange("p a t -> p (a t)")[:, 0:5 * D].rearrange("p (w d) -> p w d", w=5)
    b4s = sb("b4s", [128, 4])
    vbc = sb("vbc", [128, 4, D])
    oT = arena[:, 0:T]
    wos = sb("wos", [128, D])
    rts = sb("rts", [128, E])
    wgs = sb("wgs", [128, E, M])
    wus = sb("wus", [128, E, M])
    wds = sb("wds", [128, E, MC, D])
    pay = arena[:, 0:TOPK * TT * ROW].rearrange("p (k t c) -> p k t c", k=TOPK, c=ROW)
    xr0 = TOPK * TT * ROW
    xring = arena[:, xr0:xr0 + XR * ROW].rearrange("p (b c) -> p b c", b=XR)
    xt = hT[:, 0:2 * 128].rearrange("p (b t) -> p b t", b=2)
    obuf = hT[:, 256:256 + OR * D].rearrange("p (b d) -> p b d", b=OR)
    padrow = sb("padrow", [128, ROW])
    rowid = sb("rowid", [128, TOPK, TT], I32)
    below = sb("below", [128, 128])
    ones = sb("ones", [128, 128])
    kstep = sb("kstep", [128, TT])
    jstep = sb("jstep", [128, NSLOT])
    before = sb("before", [128, E, E])
    inti = sb("inti", [128, NSLOT + TT], I32)
    rw = sb("rw", [128, NSLOT * E])
    cnt = sb("cnt", [128, 4, E])
    posf = sb("posf", [128, TOPK, TT])
    posi = sb("posi", [128, TOPK, TT], I32)
    etf = sb("etf", [128, NSLOT])
    eti = sb("eti", [128, NSLOT], I32)
    identf = sb("identf", [128, 128])
    identb = sb("identb", [128, 128], BF16)
    mask_rows = sb("mask_rows", [128, 128], BF16)
    mask_cols = sb("mask_cols", [128, 128], BF16)
    revi = sb("revi", [128, E], mybir.dt.int32)
    rev = sb("rev", [128, E])
    stats = sb("stats", [128, TT, 6])
    mv = sb("mv", [128, TT, 2])
    rst = sb("rst", [128, 4, TT])
    mpart = sb("mpart", [128, 2, 16, NC])
    mx = sb("mx", [128, 2, 16])
    m3 = sb("m3", [16, 2, 3, 128], BF16)
    mr = sb("mr", [16, 2, 128])
    rden = sb("rden", [128, TPC, HPG, 1])
    gw = rec[:, :, :].rearrange("p a (b t e) -> p (a b) t e", t=TT, e=E)
    gs = sb("gs", [128, 6, TT])
    ps = nc.alloc_psum_tensor("ps", [128, 8, CH], F32)
    pflat = probs[:, :, :, :].rearrange("p a h t -> p (a h t)")
    sgb = [pflat[:, i * CH:i * CH + M] for i in (0, 1)]
    acb = [pflat[:, i * CH:i * CH + M] for i in (2, 3)]
    atb = [pflat[0:MR, i * CH:(i + 1) * CH].rearrange("p (c t) -> p c t", c=MC) for i in (4, 5)]

    split = nc.dram_tensor("split", [2, 3, 128, T], BF16, kind="Internal").ap()

    guard = nc.dram_tensor("guard", [2, 3, 16, 128], BF16, kind="Internal").ap()

    sent = nc.dram_tensor("sent", [NSLOT * 128, ROW], F32, kind="Internal").ap()
    results = nc.dram_tensor("results", [TOPK * T, D], F32, kind="Internal").ap()

    sems = []
    def sem(name):
        s = nc.alloc_semaphore(name)
        sems.append(s)
        return s

    load_s = sem("load_s")
    const_s = sem("const_s")
    dve_s = sem("dve_s")
    pool_s = sem("pool_s")
    var_s = sem("var_s")
    std_s = sem("std_s")
    hn_s = sem("hn_s")
    htp_s = sem("htp_s")
    ht_s = sem("ht_s")
    proj_s = sem("proj_s")
    rope_s = sem("rope_s")
    y_s = sem("y_s")
    y0_s = sem("y0_s")
    r_s = sem("r_s")
    y1_s = sem("y1_s")
    y2_s = sem("y2_s")
    vp_s = sem("vp_s")
    vv_s = sem("vv_s")
    st_s = [sem("st0_s"), sem("st1_s")]
    par_s = sem("par_s")
    zero_s = sem("zero_s")
    ot0_s = sem("ot0_s")
    ld_s = [sem(f"ld{g}_s") for g in range(NG)]
    scores_s = sem("scores_s")
    exp_s = sem("exp_s")
    pv_s = sem("pv_s")
    mm_s = sem("mm_s")
    mfree_s = sem("mfree_s")
    mx_s = sem("mx_s")
    m3_s = sem("m3_s")
    mrow_s = [sem("mrow0_s"), sem("mrow1_s")]
    gd_s = [sem("gd0_s"), sem("gd1_s")]
    otf_s = sem("otf_s")
    rec_s = sem("rec_s")
    otn_s = sem("otn_s")
    dvb_s = sem("dvb_s")
    otp_s = sem("otp_s")
    ot_s = sem("ot_s")
    wo_s = sem("wo_s")
    dvc_s = sem("dvc_s")
    x2_s = sem("x2_s")
    ms_s = sem("ms_s")
    sd2_s = sem("sd2_s")
    h2_s = sem("h2_s")
    h2p_s = sem("h2p_s")
    h2t_s = sem("h2t_s")
    lg_s = sem("lg_s")
    mxl_s = sem("mxl_s")
    ex_s = sem("ex_s")
    rk_s = sem("rk_s")
    rank_s = sem("rank_s")
    payw_s = sem("payw_s")
    reset_s = sem("reset_s")
    x_s = [sem(f"tile{k}_s") for k in range(XR)]
    xtp_s = sem("xtp_s")
    xt_s = sem("xt_s")
    gu_s = sem("gu_s")
    sg_s = sem("sg_s")
    ac_s = sem("ac_s")
    tp_s = sem("tp_s")
    at_s = sem("at_s")
    dn_s = sem("dn_s")
    ob_s = sem("ob_s")
    sent_s = sem("sent_s")
    res_s = [sem(f"res{k}_s") for k in range(OR)]
    fin_s = [sem(f"fin{k}_s") for k in range(TOPK)]
    end_s = sem("end_s")
    swdge_sems = range(sent_s.num, res_s[-1].num + 1)
    all_sems = range(min(s.num for s in sems), max(s.num for s in sems) + 1)
    assert len(all_sems) == len(sems)

    chunks, events = core_schedule()

    def group_end(g):
        return 2 * sum(TPC * (c + 1) for gg, c in chunks if gg <= g)

    pbuf = arena[:, 8 * CH:11 * CH].bitcast(BF16).rearrange("p (b l t) -> p b l t", b=2, l=3)

    def parts(i):
        return pbuf[:, i % 2, :, :]

    with nc.Block() as block:

        @block.sync
        def _(sp):
            sp.dma_start(xs[:, :, :], x_in.rearrange("(t p) d -> p t d", p=128)).then_inc(load_s, 16)
            sp.dma_start(rts[:, :], router).then_inc(load_s, 16)
            sp.dma_start(wgs[:, :, :], w_gate.rearrange("e d m -> d e m")).then_inc(load_s, 16)
            sp.dma_start(wus[:, :, :], w_up.rearrange("e d m -> d e m")).then_inc(load_s, 16)
            sp.dma_start(wds[0:MR, :, :, :], w_down.rearrange("e (c p) d -> p e c d", p=MR)).then_inc(load_s, 16)
            sp.wait_ge(load_s, 80)

        @block.gpsimd
        def _(pool):
            n = 0
            for tile, value in ((identf, 0.0), (identb, 0.0), (mask_rows, 0.0), (mask_cols, 0.0)):
                pool.memset(tile[:, :], value).then_inc(pool_s, 1)
                n += 1
            pool.iota(revi[:, :], pattern=[[-1, E]], base=E, channel_multiplier=0).then_inc(pool_s, 1)
            pool.iota(inti[:, 0:NSLOT], pattern=[[1, NSLOT]], base=0, channel_multiplier=0).then_inc(pool_s, 1)
            pool.iota(inti[:, NSLOT:], pattern=[[128, TT]], base=0, channel_multiplier=0).then_inc(pool_s, 1)
            pool.iota(rowid[:, :, :], pattern=[[T, TOPK], [128, TT]], base=0, channel_multiplier=1).then_inc(pool_s, 1)
            pool.memset(padrow[:, :], 0.0).then_inc(pool_s, 1)
            pool.memset(below[:, :], 0.0).then_inc(pool_s, 1)
            pool.memset(ones[:, :], 1.0).then_inc(pool_s, 1)
            pool.memset(before[:, :, :], 0.0).then_inc(pool_s, 1)
            pool.wait_ge(pool_s, n + 8)
            pool.iota(padrow[:, D + 1:D + 2].bitcast(I32), pattern=[[0, 1]], base=TOPK * T,
                      channel_multiplier=1).then_inc(const_s, 1)
            pool.affine_select(out=below[:, :], in_=below[:, :], compare_op=ALU.is_ge, fill=1.0,
                               base=0, pattern=[[-1, 128]], channel_multiplier=1).then_inc(const_s, 1)
            pool.affine_select(out=before[:, :, :], in_=before[:, :, :], compare_op=ALU.is_ge, fill=1.0,
                               base=0, pattern=[[-1, E], [1, E]], channel_multiplier=0).then_inc(const_s, 1)
            pool.tensor_copy(jstep[:, :], inti[:, 0:NSLOT]).then_inc(const_s, 1)
            pool.tensor_copy(kstep[:, :], inti[:, NSLOT:]).then_inc(const_s, 1)
            for tile in (identf, identb):
                pool.affine_select(out=tile[:, :], in_=tile[:, :], compare_op=ALU.not_equal, fill=1.0,
                                   base=0, pattern=[[-1, 128]], channel_multiplier=1).then_inc(const_s, 1)
            pool.affine_select(out=mask_rows[:, :], in_=mask_rows[:, :], compare_op=ALU.is_ge, fill=MASKED,
                               base=0, pattern=[[-1, 128]], channel_multiplier=1).then_inc(const_s, 1)
            pool.affine_select(out=mask_cols[:, :], in_=mask_cols[:, :], compare_op=ALU.is_ge, fill=MASKED,
                               base=0, pattern=[[1, 128]], channel_multiplier=-1).then_inc(const_s, 1)
            pool.tensor_copy(rev[:, :], revi[:, :]).then_inc(const_s, 1)
            pool.wait_ge(const_s, 10)

        @block.vector
        def _(dve):
            dve.memset(vv[:, :, :, :], 1.0).then_inc(dve_s, 1)
            dve.memset(ka[64:96, :, :, :], 1.0).then_inc(dve_s, 1)
            dve.wait_ge(dve_s, 2)

    nc.all_engine_barrier(sems_to_clear=all_sems)

    with nc.Fori(0, NLAYER) as layer:
        with nc.Block() as block:

            @block.sync
            def _(sp):
                one = bass.ds(layer, 1)
                sp.dma_start(w5s[:, :, :], w5[one].rearrange("o p w d -> (o p) w d")).then_inc(par_s, 16)
                sp.dma_start(b4s[:, :], b4[one].rearrange("o p w -> (o p) w")).then_inc(par_s, 16)
                sp.dma_start(vbc[:, :, :].rearrange("p v d -> p (v d)"),
                             vecs[one].broadcast_to([128, 4 * D])).then_inc(par_s, 16)
                sp.dma_start(wos[:, :], wo_w[one].rearrange("o p d -> (o p) d")).then_inc(par_s, 16)
                sp.dma_start(rtab, rope[one].rearrange("o p a t -> (o p) a t")).then_inc(par_s, 16)
                for i in range(2 * NC):
                    c, which = i // 2, i % 2
                    sp.wait_ge(y2_s, i + 1)
                    sp.dma_start(split[which, :, :, c * CH:(c + 1) * CH].rearrange("l p t -> p l t"),
                                 parts(i)).then_inc(st_s[i % 2], 16)
                for k in (0, 1):
                    sp.wait_ge(st_s[k], 16 * NC)

            @block.vector
            def _(dve):
                n = [0]

                def link(ins):
                    n[0] += 1
                    ins.then_inc(dve_s, 1)
                    dve.wait_ge(dve_s, n[0])

                for t in range(TT):
                    ins = dve.bn_stats(stats[:, t, :], xs[:, t, :])
                link(ins)
                for t in range(TT):
                    ins = dve.bn_aggr(mv[:, t, :], stats[:, t, :])
                link(ins)
                dve.tensor_scalar(rst[:, 0, :], mv[:, :, 1], LN_EPS, None, ALU.add).then_inc(var_s, 1)
                dve.wait_ge(std_s, 1)
                link(dve.reciprocal(rst[:, 1, :], rst[:, 0, :]))
                for t in range(TT):
                    ins = dve.tensor_scalar(x1[:, t, :], xs[:, t, :], mv[:, t, 0:1], rst[:, 1, t:t + 1],
                                            ALU.subtract, ALU.mult)
                link(ins)
                for t in range(TT):
                    ins = dve.tensor_tensor_reduce(hn[:, t, :], x1[:, t, :], x1[:, t, :], 1.0, 0.0,
                                                   ALU.mult, ALU.add, rst[:, 2, t:t + 1])
                link(ins)
                dve.tensor_scalar(rst[:, 2, :], rst[:, 2, :], 1.0 / D, RMS_EPS, ALU.mult, ALU.add).then_inc(var_s, 1)
                dve.wait_ge(std_s, 2)
                link(dve.reciprocal(rst[:, 3, :], rst[:, 2, :]))
                with dve.If(layer == 1):
                    dve.memset(rst[:, 0, :], 1.0).then_inc(dve_s, 1)
                with dve.If(layer != 1):
                    dve.tensor_copy(rst[:, 0, :], rst[:, 3, :]).then_inc(dve_s, 1)
                n[0] += 1
                dve.wait_ge(dve_s, n[0])
                dve.wait_ge(par_s, 80)
                for t in range(TT):
                    dve.scalar_tensor_tensor(hn[:, t, :], x1[:, t, :], rst[:, 0, t:t + 1], vbc[:, V_LN1, :],
                                             ALU.mult, ALU.mult).then_inc(hn_s, 1)

                def remainder(i):
                    dve.wait_ge(y0_s, i + 1)
                    dve.tensor_tensor(tmp(6 + i % 2), tmp(4 + i % 2), parts(i)[:, 0, :], ALU.subtract).then_inc(r_s, 1)

                for c in range(NC):
                    cols = slice(c * CH, (c + 1) * CH)
                    for which in (0, 1):
                        i = 2 * c + which
                        if i >= 2:
                            dve.wait_ge(y_s, i - 1)
                        for k in (0, 1):
                            dve.wait_ge(proj_s, 2 * i + k + 1)
                            dve.scalar_tensor_tensor(tmp(2 * (i % 2) + k), ps[:, 2 + 2 * which + k, :],
                                                     b4s[:, 2 * which + k:2 * which + k + 1], rtab[:, k, cols],
                                                     ALU.add, ALU.mult).then_inc(rope_s, 1)
                        if i:
                            if i >= 3:
                                dve.wait_ge(y2_s, i - 2)
                            remainder(i - 1)
                    dve.wait_ge(vp_s, c + 1)
                    dve.tensor_tensor(vv[:, TPC * c:TPC * (c + 1), :, 0:HD],
                                      ps[:, 6 + c % 2, :].rearrange("p (t h d) -> p t h d", t=TPC, h=H),
                                      vbc[:, V_BV:V_BV + 1, :].rearrange("p o (h d) -> p o h d", h=H).broadcast_to(
                                          [128, TPC, H, HD]), ALU.add).then_inc(vv_s, 1)
                dve.wait_ge(y2_s, 2 * NC - 2)
                remainder(2 * NC - 1)

            @block.gpsimd
            def _(pool):
                def third(i):
                    pool.wait_ge(y1_s, i + 1)
                    pool.tensor_tensor(parts(i)[:, 2, :], tmp(6 + i % 2), parts(i)[:, 1, :],
                                       ALU.subtract).then_inc(y2_s, 1)

                for i in range(2 * NC):
                    pool.wait_ge(rope_s, 2 * i + 2)
                    if i >= 2:
                        pool.wait_ge(r_s, i - 1)
                    pool.tensor_tensor(tmp(4 + i % 2), tmp(2 * (i % 2)), tmp(2 * (i % 2) + 1),
                                       ALU.add).then_inc(y_s, 1)
                    if i:
                        third(i - 1)
                third(2 * NC - 1)

            @block.scalar
            def _(act):
                act.wait_ge(var_s, 1)
                act.activation(rst[:, 0, :], rst[:, 0, :], ACT.Sqrt).then_inc(std_s, 1)
                act.wait_ge(var_s, 2)
                act.activation(rst[:, 2, :], rst[:, 2, :], ACT.Sqrt).then_inc(std_s, 1)

                def second(i):
                    act.wait_ge(r_s, i + 1)
                    act.activation(parts(i)[:, 1, :], tmp(6 + i % 2), ACT.Copy).then_inc(y1_s, 1)

                for c in range(NC):
                    act.wait_ge(htp_s, c + 1)
                    act.activation(hT[:, c * CH:(c + 1) * CH], ps[:, c % 2, :], ACT.Copy).then_inc(ht_s, 1)
                    for i in (2 * c, 2 * c + 1):
                        act.wait_ge(y_s, i + 1)
                        if i >= 2:
                            act.wait_ge(st_s[i % 2], 16 * (i // 2))
                        act.activation(parts(i)[:, 0, :], tmp(4 + i % 2), ACT.Copy).then_inc(y0_s, 1)
                        if i:
                            second(i - 1)
                second(2 * NC - 1)

            @block.tensor
            def _(pe):
                for c in range(NC):
                    for k in range(TPC):
                        t = TPC * c + k
                        pe.wait_ge(hn_s, t + 1)
                        if c >= 2:
                            pe.wait_ge(ht_s, c - 1)
                        ins = pe.transpose(ps[:, c % 2, k * 128:(k + 1) * 128], hn[:, t, :], identf[:, :])
                    ins.then_inc(htp_s, 1)
                    pe.wait_ge(ht_s, c + 1)
                    pe.wait_ge(par_s, 80)
                    for w in range(4):
                        if c:
                            pe.wait_ge(rope_s, 4 * (c - 1) + w + 1)
                        pe.matmul(ps[:, 2 + w, :], w5s[:, w, :], hT[:, c * CH:(c + 1) * CH],
                                  start=True, stop=True).then_inc(proj_s, 1)
                    if c >= 2:
                        pe.wait_ge(vv_s, c - 1)
                    for k in range(TPC):
                        t = TPC * c + k
                        ins = pe.matmul(ps[:, 6 + c % 2, k * 128:(k + 1) * 128], hT[:, t * 128:(t + 1) * 128],
                                        w5s[:, W_V, :], start=True, stop=True)
                    ins.then_inc(vp_s, 1)

        with nc.Block() as block:

            @block.sync
            def _(sp):
                def load(g):
                    b = g % 2
                    sp.wait_ge(zero_s, g + 1)
                    if g >= 2:
                        sp.wait_ge(scores_s, group_end(g - 2))
                    for s in range(9):
                        for which, level, dst in ((0, s % 3, qa), (1, s // 3, ka)):
                            src = split[which, level, g * HPG * HD:(g + 1) * HPG * HD, :]
                            sp.dma_start(dst[s * HD:(s + 1) * HD, b, :, :],
                                         src.rearrange("(h i) t -> i h t", i=HD)).then_inc(ld_s[g], 16)

                load(0)
                load(1)
                sp.dma_start(sent.rearrange("(j p) c -> p j c", p=128),
                             padrow[:, :].rearrange("p (o c) -> p o c", o=1).broadcast_to([128, NSLOT, ROW])
                             ).then_inc(reset_s, 16)
                for ev in events:
                    if ev[0] == "maxout":
                        j = ev[1]
                        g, c = chunks[j]
                        sp.wait_ge(m3_s, j + 1)
                        if j >= 2:
                            sp.wait_ge(mrow_s[j % 2], 16 * (j // 2))
                        sp.dma_start(guard[j % 2].rearrange("l r t -> r l t"), m3[:, j % 2, :, :]).then_inc(gd_s[j % 2], 16)
                        sp.wait_ge(gd_s[j % 2], 16 * (j // 2 + 1))
                        sp.dma_start(qa[GUARD:GUARD + 3, g % 2, :, c * CH:(c + 1) * CH],
                                     guard[j % 2].rearrange("l (h q) t -> l h (q t)", h=HPG)).then_inc(mrow_s[j % 2], 16)
                    elif ev[0] == "reload" and ev[1] + 2 < NG:
                        load(ev[1] + 2)

                sp.wait_ge(reset_s, 16)

            @block.tensor
            def _(pe):
                mi = 0
                pe.wait_ge(ot0_s, 1)
                for ev in events:
                    kind = ev[0]
                    if kind in ("rowmax", "maxout", "normalise"):
                        bank = 4 + mi % 2
                        if mi >= 2:
                            pe.wait_ge(mfree_s, mi - 1)
                        mi += 1
                    if kind == "rowmax":
                        _, j, qt, h, kc = ev
                        g, c = chunks[j]
                        b = g % 2
                        if qt == 0 and h == 0 and kc == 0:
                            pe.wait_ge(ld_s[g], 16 * 18)
                        tile = TPC * c + qt
                        n = min(CH, (tile + 1) * 128 - kc * CH)
                        diag = kc == c
                        ins = pe.matmul(ps[:, bank, 0:n], qa[0:KROWS, b, h, tile * 128:(tile + 1) * 128],
                                        ka[0:KROWS, b, h, kc * CH:kc * CH + n], start=True, stop=not diag)
                        if diag:
                            ins = pe.matmul(ps[:, bank, n - 128:n], identb[:, :], mask_rows[:, :],
                                            start=False, stop=True)
                        ins.then_inc(mm_s, 1)
                    elif kind == "maxout":
                        j = ev[1]
                        pe.wait_ge(mx_s, j + 1)
                        pe.transpose(ps[0:16, bank, 0:128], mx[:, j % 2, :], identf[:, :]).then_inc(mm_s, 1)
                    elif kind == "normalise":
                        j = ev[1]
                        pe.wait_ge(otf_s, j + 1)
                        for k in range(TPC):
                            ins = pe.transpose(ps[:, bank, k * 128:(k + 1) * 128],
                                               otf[:, j % 2, k * 128:(k + 1) * 128], identf[:, :])
                        ins.then_inc(mm_s, 1)
                    elif kind == "scores":
                        _, s, j, kt, pair = ev
                        g, c = chunks[j]
                        b = g % 2
                        if kt == 0 and pair == 0:
                            pe.wait_ge(mrow_s[j % 2], 16 * (j // 2 + 1))
                        q0 = max(0, kt - TPC * c) * 128
                        n = CH - q0
                        diag = kt >= TPC * c
                        u = 2 * s + pair
                        if u >= 2:
                            pe.wait_ge(exp_s, u - 1)
                        for k in (0, 1):
                            h = 2 * pair + k
                            dst = ps[:, 2 * (u % 2) + k, 0:n]
                            ins = pe.matmul(dst, ka[0:KROWS, b, h, kt * 128:(kt + 1) * 128],
                                            qa[0:KROWS, b, h, c * CH + q0:(c + 1) * CH],
                                            start=True, stop=not diag)
                            if diag:
                                ins = pe.matmul(dst[:, 0:128], identb[:, :], mask_cols[:, :],
                                                start=False, stop=True)
                        ins.then_inc(scores_s, 1)
                    elif kind == "values":
                        _, s, j, kt = ev
                        g, c = chunks[j]
                        q0 = max(0, kt - TPC * c) * 128
                        pe.wait_ge(exp_s, 2 * s + 2)
                        if kt == 0 and j >= 2:
                            pe.wait_ge(otf_s, j - 1)
                        for h in range(HPG):
                            ins = pe.matmul(ps[32 * h:32 * h + HD + 1, 6 + j % 2, q0:CH],
                                            vv[:, kt, g * HPG + h, :], probs[:, s % 2, h, 0:CH - q0],
                                            start=kt == 0, stop=kt == TPC * (c + 1) - 1)
                        ins.then_inc(pv_s, 1)

            @block.scalar
            def _(act):
                for ev in events:
                    if ev[0] == "scores":
                        _, s, j, kt, pair = ev
                        g, c = chunks[j]
                        n = CH - max(0, kt - TPC * c) * 128
                        u = 2 * s + pair
                        if s >= 2 and pair == 0:
                            act.wait_ge(pv_s, s - 1)
                        act.wait_ge(scores_s, u + 1)
                        act.activation(probs[:, s % 2, 2 * pair:2 * pair + 2, 0:n],
                                       ps[:, 2 * (u % 2):2 * (u % 2) + 2, 0:n], ACT.Exp,
                                       scale=SCALE).then_inc(exp_s, 1)
                    elif ev[0] == "evacuate":
                        j = ev[1]
                        act.wait_ge(pv_s, sum(TPC * (c + 1) for _, c in chunks[:j + 1]))
                        if j >= 2:
                            act.wait_ge(otn_s, j - 1)
                        act.activation(otf[:, j % 2, :], ps[:, 6 + j % 2, :], ACT.Copy).then_inc(otf_s, 1)

            @block.vector
            def _(dve):
                dve.memset(ps[:, 6:8, :], 0.0).then_inc(ot0_s, 1)
                mi = 0
                n = [0]

                def link(ins):
                    n[0] += 1
                    ins.then_inc(dvb_s, 1)
                    dve.wait_ge(dvb_s, n[0])

                for ev in events:
                    kind = ev[0]
                    if kind in ("rowmax", "maxout", "normalise"):
                        bank = 4 + mi % 2
                        mi += 1
                        dve.wait_ge(mm_s, mi)
                    if kind == "rowmax":
                        _, j, qt, h, kc = ev
                        g, c = chunks[j]
                        w = min(CH, (TPC * c + qt + 1) * 128 - kc * CH)
                        dve.tensor_reduce(mpart[:, j % 2, 4 * h + qt, kc:kc + 1], ps[:, bank, 0:w],
                                          axis=AX.X, op=ALU.max).then_inc(mfree_s, 1)
                        if qt == TPC - 1 and h == HPG - 1 and kc == c:
                            dve.wait_ge(mfree_s, mi)
                            if j >= 2:
                                dve.wait_ge(m3_s, j - 1)
                            dve.tensor_reduce(mx[:, j % 2, :], mpart[:, j % 2, :, 0:c + 1], axis=AX.X,
                                              op=ALU.max, negate=True).then_inc(mx_s, 1)
                    elif kind == "maxout":
                        j = ev[1]
                        if j >= 2:
                            dve.wait_ge(mrow_s[j % 2], 16 * (j // 2))
                        src = ps[0:16, bank, 0:128]
                        link(dve.tensor_copy(m3[:, j % 2, 0, :], src))
                        dve.tensor_tensor(mr[:, 0, :], src, m3[:, j % 2, 0, :], ALU.subtract).then_inc(mfree_s, 1)
                        dve.wait_ge(mfree_s, mi)
                        link(dve.tensor_copy(m3[:, j % 2, 1, :], mr[:, 0, :]))
                        dve.tensor_tensor(m3[:, j % 2, 2, :], mr[:, 0, :], m3[:, j % 2, 1, :],
                                          ALU.subtract).then_inc(m3_s, 1)
                    elif kind == "normalise":
                        j = ev[1]
                        g, c = chunks[j]
                        turned = ps[:, bank, :].rearrange("p (q h r) -> p q h r", q=TPC, r=32)
                        link(dve.reciprocal(rden[:, :, :, :], turned[:, :, :, HD:HD + 1]))
                        dve.tensor_tensor(
                            onat[:, TPC * c:TPC * (c + 1), 32 * g:32 * g + 32].rearrange("p q (h i) -> p q h i", i=HD),
                            turned[:, :, :, 0:HD], rden[:, :, :, :].broadcast_to([128, TPC, HPG, HD]),
                            ALU.mult).then_inc(mfree_s, 1)
                        dve.wait_ge(mfree_s, mi)
                        dve.engine_nop().then_inc(otn_s, 1)

            @block.gpsimd
            def _(pool):
                zeros = lambda b: qa[64:96, b, :, :].rearrange("p h t -> p (h t)").bitcast(F32)
                pool.memset(zeros(0), 0.0).then_inc(zero_s, 1)
                pool.memset(zeros(1), 0.0).then_inc(zero_s, 1)
                pool.wait_ge(zero_s, 2)
                for ev in events:
                    if ev[0] == "reload" and ev[1] + 2 < NG:
                        pool.wait_ge(scores_s, group_end(ev[1]))
                        pool.memset(zeros(ev[1] % 2), 0.0).then_inc(zero_s, 1)
                        pool.wait_ge(zero_s, ev[1] + 3)

        with nc.Block() as block:

            @block.tensor
            def _(pe):
                def project(c):
                    pe.wait_ge(ot_s, c + 1)
                    if c >= 2:
                        pe.wait_ge(x2_s, c - 1)
                    for k in range(TPC):
                        t = TPC * c + k
                        ins = pe.matmul(ps[:, 2 + c % 2, k * 128:(k + 1) * 128], oT[:, t * 128:(t + 1) * 128],
                                        wos[:, :], start=True, stop=True)
                    ins.then_inc(wo_s, 1)

                for c in range(NC):
                    if c >= 2:
                        pe.wait_ge(ot_s, c - 1)
                    for k in range(TPC):
                        ins = pe.transpose(ps[:, c % 2, k * 128:(k + 1) * 128], onat[:, TPC * c + k, :], identf[:, :])
                    ins.then_inc(otp_s, 1)
                    if c:
                        project(c - 1)
                project(NC - 1)
                for c in range(NC):
                    if c >= 2:
                        pe.wait_ge(h2t_s, c - 1)
                    for k in range(TPC):
                        t = TPC * c + k
                        pe.wait_ge(h2_s, t + 1)
                        ins = pe.transpose(ps[:, 4 + c % 2, k * 128:(k + 1) * 128], pay[:, 0, t, 0:D], identf[:, :])
                    ins.then_inc(h2p_s, 1)
                for t in range(TT):
                    pe.wait_ge(h2t_s, t // TPC + 1)
                    ins = pe.matmul(ps[:, 6, t * E:(t + 1) * E], hT[:, t * 128:(t + 1) * 128], rts[:, :],
                                    start=True, stop=True)
                ins.then_inc(lg_s, 1)
                pe.wait_ge(rk_s, 1)
                taken = gw[:, 5, :, :].rearrange("p t e -> p (t e)")
                pe.matmul(ps[:, 7, 0:TT * E], below[:, :], taken, start=True, stop=True)
                pe.matmul(ps[:, 7, TT * E:2 * TT * E], ones[:, :], taken, start=True, stop=True).then_inc(rank_s, 1)

            @block.scalar
            def _(act):
                for c in range(NC):
                    act.wait_ge(otp_s, c + 1)
                    act.activation(oT[:, c * CH:(c + 1) * CH], ps[:, c % 2, :], ACT.Copy).then_inc(ot_s, 1)
                act.wait_ge(ms_s, 1)
                act.activation(rst[:, 2, :], rst[:, 2, :], ACT.Sqrt).then_inc(sd2_s, 1)
                for c in range(NC):
                    act.wait_ge(h2p_s, c + 1)
                    act.activation(hT[:, c * CH:(c + 1) * CH], ps[:, 4 + c % 2, :], ACT.Copy).then_inc(h2t_s, 1)
                act.wait_ge(mxl_s, 1)
                act.activation(gw[:, 0, :, :], gw[:, 0, :, :], ACT.Exp).then_inc(ex_s, 1)

            @block.vector
            def _(dve):
                n = [0]

                def link(ins):
                    n[0] += 1
                    ins.then_inc(dvc_s, 1)
                    dve.wait_ge(dvc_s, n[0])

                for c in range(NC):
                    dve.wait_ge(wo_s, c + 1)
                    rows = slice(TPC * c, TPC * (c + 1))
                    link(dve.tensor_tensor(rec[:, 0, :].rearrange("p (t d) -> p t d", d=D),
                                           ps[:, 2 + c % 2, :].rearrange("p (t d) -> p t d", d=D),
                                           vbc[:, V_BO:V_BO + 1, :].broadcast_to([128, TPC, D]), ALU.add))
                    y = rec[:, 0, :].rearrange("p (t d) -> p t d", d=D)
                    with dve.If(layer == 1):
                        dve.tensor_tensor(xs[:, rows, :], xs[:, rows, :], y, ALU.add).then_inc(x2_s, 1)
                    with dve.If(layer != 1):
                        dve.tensor_tensor(x1[:, rows, :], x1[:, rows, :], y, ALU.add).then_inc(x2_s, 1)
                    dve.wait_ge(x2_s, c + 1)
                for t in range(TT):
                    ins = dve.tensor_tensor_reduce(hn[:, t, :], x1[:, t, :], x1[:, t, :], 1.0, 0.0,
                                                   ALU.mult, ALU.add, rst[:, 2, t:t + 1])
                link(ins)
                dve.tensor_scalar(rst[:, 2, :], rst[:, 2, :], 1.0 / D, RMS_EPS, ALU.mult, ALU.add).then_inc(ms_s, 1)
                dve.wait_ge(sd2_s, 1)
                link(dve.reciprocal(rst[:, 3, :], rst[:, 2, :]))
                for t in range(TT):
                    dve.scalar_tensor_tensor(pay[:, 0, t, 0:D], x1[:, t, :], rst[:, 3, t:t + 1], vbc[:, V_LN2, :],
                                             ALU.mult, ALU.mult).then_inc(h2_s, 1)
                dve.wait_ge(lg_s, 1)
                lg = ps[:, 6, 0:TT * E].rearrange("p (t e) -> p t e", e=E)
                shape = [128, TT, E]

                def wide(k):
                    return gs[:, k, :].rearrange("p (t o) -> p t o", o=1).broadcast_to(shape)

                revb = rev[:, :].rearrange("p (o e) -> p o e", o=1).broadcast_to(shape)
                link(dve.tensor_reduce(gs[:, 0, :], lg, axis=AX.X, op=ALU.max))
                dve.tensor_tensor(gw[:, 0, :, :], lg, wide(0), ALU.subtract).then_inc(mxl_s, 1)
                dve.wait_ge(ex_s, 1)
                link(dve.tensor_reduce(gs[:, 1, :], gw[:, 0, :, :], axis=AX.X, op=ALU.add))
                link(dve.reciprocal(gs[:, 0, :], gs[:, 1, :]))
                link(dve.tensor_tensor(gw[:, 1, :, :], gw[:, 0, :, :], wide(0), ALU.mult))
                def pick(src, dst, peak, at):
                    link(dve.tensor_reduce(gs[:, peak, :], src, axis=AX.X, op=ALU.max))
                    link(dve.tensor_tensor(gw[:, 7, :, :], src, wide(peak), ALU.is_equal))
                    link(dve.tensor_tensor(gw[:, 7, :, :], gw[:, 7, :, :], revb, ALU.mult))
                    link(dve.tensor_reduce(gs[:, at, :], gw[:, 7, :, :], axis=AX.X, op=ALU.max))
                    link(dve.tensor_tensor(dst, revb, wide(at), ALU.is_equal))

                pick(gw[:, 1, :, :], gw[:, 2, :, :], 2, 3)
                link(dve.scalar_tensor_tensor(gw[:, 3, :, :], gw[:, 2, :, :], -2.0, gw[:, 1, :, :], ALU.mult, ALU.add))
                pick(gw[:, 3, :, :], gw[:, 4, :, :], 4, 3)
                dve.tensor_tensor(gw[:, 5, :, :], gw[:, 2, :, :], gw[:, 4, :, :], ALU.add).then_inc(rk_s, 1)
                link(dve.tensor_tensor(gs[:, 5, :], gs[:, 2, :], gs[:, 4, :], ALU.add))
                link(dve.reciprocal(gs[:, 0, :], gs[:, 5, :]))
                for k in range(TOPK):
                    dve.tensor_tensor(pay[:, k, :, D], gs[:, 2 + 2 * k, :], gs[:, 0, :], ALU.mult)
                dve.wait_ge(rank_s, 1)
                tot = gw[:, 0, :, :]
                link(dve.tensor_copy(tot, ps[:, 7, TT * E:2 * TT * E].rearrange("p (t e) -> p t e", e=E)))
                a, b = tot, 3
                step = 1
                while step < TT:
                    dst = gw[:, b, :, :]
                    dve.tensor_copy(dst[:, 0:step, :], a[:, 0:step, :])
                    link(dve.tensor_tensor(dst[:, step:TT, :], a[:, step:TT, :], a[:, 0:TT - step, :], ALU.add))
                    a, b = dst, 10 - b
                    step *= 2
                total = a[:, TT - 1:TT, :]
                link(dve.tensor_tensor(gw[:, 6, :, :], a, tot, ALU.subtract))
                over = rw[:, 0:E * TT].rearrange("p (e k) -> p e k", e=E)
                link(dve.tensor_tensor(over, total.rearrange("p o e -> p e o").broadcast_to([128, E, TT]),
                                       kstep[:, :].rearrange("p (o k) -> p o k", o=1).broadcast_to([128, E, TT]),
                                       ALU.is_gt))
                link(dve.tensor_reduce(cnt[:, 0, :], over, axis=AX.X, op=ALU.add))
                tri = rw[:, 0:E * E].rearrange("p (e f) -> p e f", e=E)
                link(dve.tensor_tensor(tri, cnt[:, 0:1, :].broadcast_to([128, E, E]), before[:, :, :], ALU.mult))
                link(dve.tensor_reduce(cnt[:, 1, :], tri, axis=AX.X, op=ALU.add))
                link(dve.tensor_tensor(cnt[:, 2, :], cnt[:, 0, :], cnt[:, 1, :], ALU.add))
                past = rw[:, 0:NSLOT * E].rearrange("p (j e) -> p j e", e=E)
                link(dve.tensor_tensor(past, jstep[:, :].rearrange("p (j o) -> p j o", o=1).broadcast_to([128, NSLOT, E]),
                                       cnt[:, 2:3, :].broadcast_to([128, NSLOT, E]), ALU.is_ge))
                link(dve.tensor_reduce(etf[:, :], past, axis=AX.X, op=ALU.add))
                dve.tensor_scalar(eti[:, :], etf[:, :], float(E - 1), None, ALU.min)
                link(dve.tensor_scalar(cnt[:, 3, :], cnt[:, 1, :], 128.0, None, ALU.mult))
                link(dve.tensor_tensor(gw[:, 6, :, :], gw[:, 6, :, :], cnt[:, 3:4, :].broadcast_to([128, TT, E]), ALU.add))
                link(dve.tensor_tensor(gw[:, 6, :, :], gw[:, 6, :, :],
                                       ps[:, 7, 0:TT * E].rearrange("p (t e) -> p t e", e=E), ALU.add))
                link(dve.tensor_tensor(gw[:, 3, :, :], gw[:, 6, :, :], gw[:, 2, :, :], ALU.mult))
                link(dve.tensor_tensor(gw[:, 7, :, :], gw[:, 6, :, :], gw[:, 4, :, :], ALU.mult))
                dve.tensor_reduce(posf[:, 0, :], gw[:, 3, :, :], axis=AX.X, op=ALU.add)
                link(dve.tensor_reduce(posf[:, 1, :], gw[:, 7, :, :], axis=AX.X, op=ALU.add))
                link(dve.tensor_copy(posi[:, :, :], posf[:, :, :]))

            @block.gpsimd
            def _(pool):
                pool.wait_ge(h2_s, TT)
                for k in range(TOPK):
                    pool.tensor_copy(pay[:, k, :, D + 1].bitcast(I32), rowid[:, k, :])
                pool.tensor_copy(pay[:, 1, :, 0:D], pay[:, 0, :, 0:D])

        with nc.Block() as block:

            @block.gpsimd
            def _(pool):
                with pool.If(layer != 1):
                    for k in range(TOPK):
                        for t in range(TT):
                            pool.indirect_dma_start(sent, bass.IndirectOffsetOnAxis(ap=posi[:, k, t:t + 1], axis=0),
                                                    pay[:, k, t, :], None).then_inc(sent_s, 16)
                    for u in range(NSLOT):
                        pool.wait_ge(ob_s, u + 1)
                        pool.indirect_dma_start(
                            results,
                            bass.IndirectOffsetOnAxis(ap=xring[:, u % XR, D + 1:D + 2].bitcast(I32), axis=0),
                            obuf[:, u % OR, :], None, bounds_check=TOPK * T - 1,
                            oob_is_err=False).then_inc(res_s[u % OR], 16)
                    pool.wait_ge(sent_s, 16 * TOPK * TT)
                    for k in range(OR):
                        pool.wait_ge(res_s[k], 16 * len(range(k, NSLOT, OR)))
                    pool.dma_reset(swdge_sems)

            @block.sync
            def _(sp):
                with sp.If(layer != 1):
                    sp.wait_ge(sent_s, 16 * TOPK * TT)
                    for u in range(NSLOT):
                        if u >= XR:
                            v = u - XR
                            sp.wait_ge(res_s[v % OR], 16 * (v // OR + 1))
                        sp.dma_start(xring[:, u % XR, :], sent[u * 128:(u + 1) * 128, :]).then_inc(x_s[u % XR], 16)
                    for k in range(OR):
                        sp.wait_ge(res_s[k], 16 * len(range(k, NSLOT, OR)))
                    for k in range(TOPK):
                        sp.dma_start(arena[:, k * T:(k + 1) * T].rearrange("p (t d) -> p t d", d=D),
                                     results[k * T:(k + 1) * T, :].rearrange("(t p) d -> p t d", p=128)
                                     ).then_inc(fin_s[k], 16)

            @block.tensor
            def _(pe):
                def turn(u):
                    pe.wait_ge(x_s[u % XR], 16 * (u // XR + 1))
                    if u:
                        pe.wait_ge(xt_s, u)
                    pe.transpose(ps[:, 7, 0:128], xring[:, u % XR, 0:D], identf[:, :]).then_inc(xtp_s, 1)

                with pe.If(layer != 1):
                    turn(0)
                    experts = []
                    for i in range(NSLOT + 2):
                        if i + 1 < NSLOT:
                            turn(i + 1)
                        if i < NSLOT:
                            expert = pe.value_load(eti[0:1, i:i + 1], min_val=0, max_val=E - 1)
                            experts.append(expert)
                            pe.wait_ge(xt_s, i + 1)
                            if i >= 2:
                                pe.wait_ge(ac_s, i - 1)
                            for k, w in ((0, wgs), (1, wus)):
                                pe.matmul(ps[:, 2 * (i % 2) + k, 0:M], xt[:, i % 2, :],
                                          w[:, bass.ds(expert, 1), :].rearrange("p o m -> p (o m)"),
                                          start=True, stop=True).then_inc(gu_s, 1)
                        if 1 <= i <= NSLOT:
                            u = i - 1
                            pe.wait_ge(ac_s, u + 1)
                            if u >= 2:
                                pe.wait_ge(at_s, u - 1)
                            for k in range(MC):
                                ins = pe.transpose(ps[0:MR, 4 + u % 2, k * 128:(k + 1) * 128],
                                                   acb[u % 2][:, k * MR:(k + 1) * MR], identf[:, :])
                            ins.then_inc(tp_s, 1)
                        if i >= 2:
                            u = i - 2
                            pe.wait_ge(at_s, u + 1)
                            if u:
                                pe.wait_ge(ob_s, u)
                            for k in range(MC):
                                ins = pe.matmul(ps[:, 6, 0:D], atb[u % 2][:, k, :],
                                                wds[0:MR, bass.ds(experts[u], 1), k, :].rearrange("p o d -> p (o d)"),
                                                start=k == 0, stop=k == MC - 1)
                            ins.then_inc(dn_s, 1)

            @block.scalar
            def _(act):
                def copy_turned(u):
                    act.wait_ge(xtp_s, u + 1)
                    if u >= 2:
                        act.wait_ge(gu_s, 2 * (u - 1))
                    act.activation(xt[:, u % 2, :], ps[:, 7, 0:128], ACT.Copy).then_inc(xt_s, 1)

                with act.If(layer != 1):
                    copy_turned(0)
                    for i in range(NSLOT + 1):
                        if i + 1 < NSLOT:
                            copy_turned(i + 1)
                        if i < NSLOT:
                            act.wait_ge(gu_s, 2 * i + 1)
                            if i >= 2:
                                act.wait_ge(ac_s, i - 1)
                            act.activation(sgb[i % 2], ps[:, 2 * (i % 2), 0:M], ACT.Silu).then_inc(sg_s, 1)
                        if i:
                            u = i - 1
                            act.wait_ge(tp_s, u + 1)
                            if u >= 2:
                                act.wait_ge(dn_s, u - 1)
                            act.activation(atb[u % 2], ps[0:MR, 4 + u % 2, :].rearrange("p (c t) -> p c t", c=MC),
                                           ACT.Copy).then_inc(at_s, 1)

            @block.vector
            def _(dve):
                with dve.If(layer != 1):
                    for i in range(NSLOT + 2):
                        if i < NSLOT:
                            dve.wait_ge(x_s[i % XR], 16 * (i // XR + 1))
                            dve.wait_ge(sg_s, i + 1)
                            dve.wait_ge(gu_s, 2 * i + 2)
                            if i >= 2:
                                dve.wait_ge(tp_s, i - 1)
                            dve.scalar_tensor_tensor(acb[i % 2], sgb[i % 2], xring[:, i % XR, D:D + 1],
                                                     ps[:, 2 * (i % 2) + 1, 0:M], ALU.mult, ALU.mult).then_inc(ac_s, 1)
                        if i >= 2:
                            u = i - 2
                            dve.wait_ge(dn_s, u + 1)
                            if u >= OR:
                                dve.wait_ge(res_s[u % OR], 16 * (u // OR))
                            dve.tensor_copy(obuf[:, u % OR, :], ps[:, 6, 0:D]).then_inc(ob_s, 1)
                    flat = x1[:, :, :].rearrange("p t d -> p (t d)")
                    for k in range(TOPK):
                        dve.wait_ge(fin_s[k], 16)
                        dve.tensor_tensor(flat, flat, arena[:, k * T:(k + 1) * T], ALU.add).then_inc(end_s, 1)
                        dve.wait_ge(end_s, k + 1)
                    dve.scalar_tensor_tensor(xs[:, :, :].rearrange("p t d -> p (t d)"), flat, 0.5,
                                             xs[:, :, :].rearrange("p t d -> p (t d)"),
                                             ALU.mult, ALU.add).then_inc(end_s, 1)

        nc.all_engine_barrier(sems_to_clear=all_sems)

    with nc.Block() as block:

        @block.sync
        def _(sp):
            sp.dma_start(out.rearrange("(t p) d -> p t d", p=128), xs[:, :, :]).then_inc(load_s, 16)
            sp.wait_ge(load_s, 16)


def rotary_tables():
    i = np.arange(HD // 2, dtype=np.float32)
    pos = np.arange(T, dtype=np.float32)
    ffn = pos[:, None] * (np.float32(1.0) / np.float32(10000.0) ** (2 * i / np.float32(HD)))[None, :]
    att = pos[:, None] * (np.float32(10000.0) ** (np.float32(-2.0) * i / np.float32(HD)))[None, :]
    tabs = []
    for angle, sign in ((ffn, -1.0), (att, 1.0), (ffn, -1.0)):
        angle = angle.astype(np.float32)
        cos, sin = np.cos(angle), np.sin(angle)
        c8 = np.concatenate([cos, cos], 1).T
        s8 = np.concatenate([np.float32(sign) * sin, sin], 1).T
        tabs.append(np.stack([np.tile(c8, (H, 1)), np.tile(s8, (H, 1))], 1))
    return np.ascontiguousarray(np.stack(tabs).astype(np.float32))


def kernel(**inputs):
    import concourse.bacc as bacc
    from concourse.bass_utils import run_bass_kernel_spmd as run

    v = {k: np.asarray(a) for k, a in inputs.items()}
    f = "L0_ffn_"
    a = "L0_attn_"
    other_half = np.arange(H * HD).reshape(H, 2, HD // 2)[:, ::-1, :].reshape(-1)
    rep = H // (v[f + "wk"].shape[1] // HD)

    def heads(w):
        return np.repeat(w.reshape(D, -1, HD), rep, axis=1).reshape(D, H * HD)

    fq, fk, fv = v[f + "wq"], heads(v[f + "wk"]), heads(v[f + "wv"])
    ffn5 = np.stack([fq, fq[:, other_half], fk, fk[:, other_half], fv], 1)
    aq, ak, av = v[a + "Wq"].T, v[a + "Wk"].T, v[a + "Wv"].T
    att5 = np.stack([aq, aq, ak, ak, av], 1)
    zero, one = np.zeros(D, np.float32), np.ones(D, np.float32)
    b_ffn = np.stack([zero] * 4, 1)
    b_att = np.stack([v[a + "bq"], v[a + "bq"], v[a + "bk"], v[a + "bk"]], 1)
    v_ffn = np.concatenate([v[f + "ln1_w"], zero, zero, v[f + "ln2_w"]])
    v_att = np.concatenate([one, v[a + "bv"], v[a + "bo"], one])

    wo_f, wo_a = v[f + "wo"], v[a + "Wo"].T
    arrays = {
        "x_in": v[a + "x"].reshape(T, D),
        "w5": np.stack([ffn5, att5, ffn5]),
        "b4": np.stack([b_ffn, b_att, b_ffn]),
        "vecs": np.stack([v_ffn, v_att, v_ffn]),
        "wo_w": np.stack([wo_f, wo_a, wo_f]),
        "rope": rotary_tables(),
        "router": v[f + "router_w"],
        "w_gate": v[f + "w_gate"],
        "w_up": v[f + "w_up"],
        "w_down": v[f + "w_down"],
    }
    arrays = {k: np.ascontiguousarray(b) for k, b in arrays.items()}
    nc = bacc.Bacc("TRN2", target_bir_lowering=False, num_devices=1)
    args = [nc.dram_tensor(k, b.shape, mybir.dt.from_np(b.dtype), kind="ExternalInput").ap() for k, b in arrays.items()]
    out = nc.dram_tensor("out", (T, D), F32, kind="ExternalOutput").ap()
    macaron_kernel(nc, *args, out)
    r = run(nc, [arrays], core_ids=[0])
    return r.results[0]["out"].reshape(1, T, D)
```

```python
import numpy as np
import concourse.bass as bass
from concourse import mybir

F32 = mybir.dt.float32
BF16 = mybir.dt.bfloat16
I32 = mybir.dt.int32
ALU = mybir.AluOpType
ACT = mybir.ActivationFunctionType
AX = mybir.AxisListType

T, D = 2048, 128
TT = T // 128
H, HD = 16, 8
HPG = 4
NG = H // HPG
CH = 512
NC = T // CH
TPC = CH // 128
KROWS = 96
GUARD = 9 * HD
E, M = 8, 448
MC, MR = 4, 112
NLAYER = 3
SCALE = float(1.0 / np.sqrt(np.float32(HD)))
MASKED = -1e30
ONES = float(np.array([0x3F803F80], np.uint32).view(np.float32)[0])
LN_EPS, RMS_EPS = 1e-5, 1e-6
W_Q, W_QR, W_K, W_KR, W_V = range(5)
V_LN1, V_BV, V_BO, V_LN2 = range(4)
TOPK = 2
NSLOT = (TOPK * T + E * 127) // 128
ROW = D + 2
SB, MB = 3, 3
BULK = 2 * NC
PB = 3
MD = 4
XR, OR = 8, 4


def core_schedule():
    chunks = []
    for g in range(NG):
        chunks += [(g, c) for c in range(NC)]
    todo = []
    for j, (g, c) in enumerate(chunks):
        units = []
        for qt in range(TPC):
            units += [(j, qt, h, 1, kc) for h in range(HPG) for kc in range(c)]
            some = min(HPG, TPC // (qt + 1))
            units += [(j, qt, h, some, c) for h in range(0, HPG, some)]
        todo += [("rowmax",) + u + (k == len(units) - 1,) for k, u in enumerate(units)]
    steps = [(j, kt) for j, (g, c) in enumerate(chunks) for kt in range(TPC * (c + 1))]

    events = []
    hop = 215.0
    pe = dve = act = 0.0
    banks = [0.0] * MB
    turn = done = 0
    split_due, late, ready = [], [], {}
    operands = [0.0, 0.0] + [float("inf")] * (NG - 2)

    def run_late(bank):
        nonlocal pe, dve
        kind, j, at = late.pop(0)
        pe = max(pe, at, banks[bank]) + (900 if kind == "project" else 450)
        dve = max(dve, pe + hop) + {"normalise": 500, "turn": 650, "project": 2600}[kind]
        banks[bank] = dve + hop - (2000 if kind == "project" else 0)
        events.append((kind, j))
        c = j if kind != "normalise" else chunks[j][1]
        if kind == "normalise" and chunks[j][0] == NG - 1:
            late.insert(0, ("turn", c, dve + hop))
        elif kind == "turn":
            late.insert(0, ("project", c, dve + hop))

    def fill(until, now, limit=0.0):
        nonlocal pe, dve, turn, done
        forced = until is not None
        bank = turn % MB
        limit = max(limit, pe)
        if split_due and (max(split_due[0][1], banks[bank]) <= limit or
                          forced and (done == len(todo) or todo[done][1] > until)):
            j, at = split_due.pop(0)
            pe = max(pe, banks[bank], at) + 220
            dve = max(dve, pe + hop) + 1000
            banks[bank] = dve - 400 + hop
            ready[j] = dve + 5500
            events.append(("maxout", j))
        elif late and max(late[0][2], banks[bank]) <= limit:
            run_late(bank)
        else:
            if done == len(todo):
                return False
            _, j, qt, h, some, kc, final = todo[done]
            g, c = chunks[j]
            if not forced and (banks[bank] > limit or j > now + MD - 1 or operands[g] > limit):
                return False
            width = min(CH, (TPC * c + qt + 1) * 128 - kc * CH) * some
            pe = max(pe, banks[bank], operands[g]) + width / 2.4 + 3 + (56 * some if kc == c else 0)
            dve = max(dve, pe + hop) + 65 + width * 1.04
            banks[bank] = dve + hop
            events.append(todo[done])
            done += 1
            if final:
                dve += 180
                split_due.append((j, dve + hop))
        turn += 1
        return True

    def main(start, length, now):
        nonlocal pe
        while fill(None, now, start) and pe < start:
            pass
        pe = max(pe, start) + length

    exp_at = {}
    values_at = {}
    for s in range(len(steps) + 1):
        j, kt = steps[s] if s < len(steps) else (len(chunks), 0)
        if s < len(steps):
            g, c = chunks[j]
            while j not in ready:
                fill(j, j)
            n = CH - max(0, kt - TPC * c) * 128
            for h in range(HPG):
                u = HPG * s + h
                main(max(exp_at.get(u - SB, 0.0) + hop, ready[j]), n / 2.4 + 3, j)
                act = max(act, pe + hop, values_at.get(s - 2, 0.0) + hop) + 52 + n * 0.83
                exp_at[u] = act
                events.append(("scores", s, j, kt, h))
            if s and g and (c, kt) == (1, 0):
                events.append(("reload", g - 1))
                if g + 1 < NG:
                    operands[g + 1] = pe + 25000
        if s:
            pj, pk = steps[s - 1]
            n = CH - max(0, pk - TPC * chunks[pj][1]) * 128
            masking = 900 if pk >= TPC * chunks[pj][1] else 0
            main(exp_at[HPG * s - 1] + hop + masking, 4 * n / 2.4 + 60, min(j, len(chunks) - 1))
            values_at[s - 1] = pe
            events.append(("values", s - 1, pj, pk))
            if pj != j:
                events.append(("evacuate", pj))
                act = max(act, pe + hop) + 480
                late.append(("normalise", pj, act + hop))
    while late:
        run_late(turn % MB)
        turn += 1
    return chunks, events, pe


def macaron_kernel(nc, x_in, w5, b4, vecs, wo_w, rope, router, w_gate, w_up, w_down, out):
    def sb(name, shape, dt=F32):
        return nc.alloc_sbuf_tensor(name, shape, dt)

    xs = sb("xs", [128, TT, D])
    x1 = sb("x1", [128, TT, D])
    hT = sb("hT", [128, T])
    qa = sb("qa", [128, 2, HPG, T], BF16)
    ka = sb("ka", [128, 2, HPG, T], BF16)
    vv = sb("vv", [128, TT, H, HD + 1])
    probs = sb("probs", [128, 2, HPG, CH])
    rtab = probs[:, :, :, :].rearrange("p a h t -> p a (h t)")
    onat = sb("onat", [128, TT, D])
    arena = sb("arena", [128, 11 * CH])
    hn = onat

    def tmp(n):
        return arena[:, n * CH:(n + 1) * CH]

    otf = sb("otf", [128, 2, CH])
    rec = sb("rec", [128, 2, CH])
    w5s = otf[:, :, :].rearrange("p a t -> p (a t)")[:, 0:5 * D].rearrange("p (w d) -> p w d", w=5)
    b4s = sb("b4s", [128, 4])
    vbc = sb("vbc", [128, 4, D])
    wos = sb("wos", [128, D])
    rts = sb("rts", [128, E])
    wgs = sb("wgs", [128, E, M])
    wus = sb("wus", [128, E, M])
    wds = sb("wds", [128, E, MC, D])
    pay = arena[:, 0:TOPK * TT * ROW].rearrange("p (k t c) -> p k t c", k=TOPK, c=ROW)
    xr0 = TOPK * TT * ROW
    xring = arena[:, xr0:xr0 + XR * ROW].rearrange("p (b c) -> p b c", b=XR)
    xt = hT[:, 0:2 * 128].rearrange("p (b t) -> p b t", b=2)
    obuf = hT[:, 256:256 + OR * D].rearrange("p (b d) -> p b d", b=OR)
    padrow = sb("padrow", [128, ROW])
    rowid = sb("rowid", [128, TOPK, TT], I32)
    below = sb("below", [128, 128])
    ones = sb("ones", [128, 128])
    kstep = sb("kstep", [128, TT])
    jstep = sb("jstep", [128, NSLOT])
    before = sb("before", [128, E, E])
    inti = sb("inti", [128, NSLOT + TT], I32)
    rw = sb("rw", [128, NSLOT * E])
    cnt = sb("cnt", [128, 4, E])
    posf = sb("posf", [128, TOPK, TT])
    posi = sb("posi", [128, TOPK, TT], I32)
    etf = sb("etf", [128, NSLOT])
    eti = sb("eti", [128, NSLOT], I32)
    identf = sb("identf", [128, 128])
    identb = sb("identb", [128, 128], BF16)
    mask_rows = sb("mask_rows", [128, 128], BF16)
    revi = sb("revi", [128, E], mybir.dt.int32)
    rev = sb("rev", [128, E])
    stats = sb("stats", [128, TT, 6])
    mv = sb("mv", [128, TT, 2])
    rst = sb("rst", [128, 4, TT])
    mpart = sb("mpart", [128, MD, HPG, TPC, NC])
    mx = sb("mx", [128, MD, 16])
    m3 = arena[0:16, CH:CH + MD * 3 * 64].bitcast(BF16).rearrange("p (j l t) -> p j l t", j=MD, l=3)
    mr = arena[0:16, 0:128]
    rden = sb("rden", [128, TPC, HPG, 1])
    gw = rec[:, :, :].rearrange("p a (b t e) -> p (a b) t e", t=TT, e=E)
    gs = sb("gs", [128, 6, TT])
    ps = nc.alloc_psum_tensor("ps", [128, 8, CH], F32)
    pflat = probs[:, :, :, :].rearrange("p a h t -> p (a h t)")
    sgb = [pflat[:, i * CH:i * CH + M] for i in (0, 1)]
    acb = [pflat[:, i * CH:i * CH + M] for i in (2, 3)]
    atb = [pflat[0:MR, i * CH:(i + 1) * CH].rearrange("p (c t) -> p c t", c=MC) for i in (4, 5)]

    qsplit = nc.dram_tensor("qsplit", [3, 128, T], BF16, kind="Internal").ap()
    ksplit = nc.dram_tensor("ksplit", [5, 128, T], BF16, kind="Internal").ap()

    guard = nc.dram_tensor("guard", [MD, 3, 16, 128], BF16, kind="Internal").ap()
    sent = nc.dram_tensor("sent", [NSLOT * 128, ROW], F32, kind="Internal").ap()
    results = nc.dram_tensor("results", [TOPK * T, D], F32, kind="Internal").ap()

    weights_loaded = nc.alloc_semaphore("weights_loaded")
    sems = []
    def sem(name):
        s = nc.alloc_semaphore(name)
        sems.append(s)
        return s

    x_loaded = sem("x_loaded")
    const_ready = sem("const_ready")
    dve_s = sem("dve_s")
    pool_s = sem("pool_s")
    variance_ready = sem("variance_ready")
    roots_ready = sem("roots_ready")
    normed = sem("normed")
    tokens_turned = sem("tokens_turned")
    tokens_copied = sem("tokens_copied")
    projected = sem("projected")
    terms_ready = sem("terms_ready")
    rotated = sem("rotated")
    part0_ready = sem("part0_ready")
    remainder_ready = sem("remainder_ready")
    part1_ready = sem("part1_ready")
    part2_ready = sem("part2_ready")
    values_projected = sem("values_projected")
    values_ready = sem("values_ready")
    parts_stored = [sem(f"parts_stored{k}") for k in range(PB)]
    params_loaded = sem("params_loaded")
    guard_zeroed = sem("guard_zeroed")
    output_zeroed = sem("output_zeroed")
    chunk_loaded = [sem(f"chunk_loaded{c}") for c in range(NC)]
    group_loaded = [sem(f"group_loaded{g}") for g in range(NG)]
    scores_ready = sem("scores_ready")
    probs_ready = sem("probs_ready")
    masked = sem("masked")
    values_weighted = sem("values_weighted")
    filler_ready = sem("filler_ready")
    filler_used = sem("filler_used")
    maxima_ready = sem("maxima_ready")
    guard_split = sem("guard_split")
    guard_ready = [sem(f"guard_ready{k}") for k in range(MD)]
    guard_stored = [sem(f"guard_stored{k}") for k in range(MD)]
    output_copied = sem("output_copied")
    output_normalised = sem("output_normalised")
    dve_core_s = sem("dve_core_s")
    dve_router_s = sem("dve_router_s")
    residual_added = sem("residual_added")
    squares_ready = sem("squares_ready")
    root_ready = sem("root_ready")
    h2_ready = sem("h2_ready")
    h2_turned = sem("h2_turned")
    h2_copied = sem("h2_copied")
    logits_ready = sem("logits_ready")
    logits_shifted = sem("logits_shifted")
    logits_exp = sem("logits_exp")
    taken_ready = sem("taken_ready")
    ranks_ready = sem("ranks_ready")
    sent_reset = sem("sent_reset")
    tile_loaded = [sem(f"tile_loaded{k}") for k in range(XR)]
    tile_turned = sem("tile_turned")
    tile_copied = sem("tile_copied")
    gate_up_ready = sem("gate_up_ready")
    silu_ready = sem("silu_ready")
    act_ready = sem("act_ready")
    act_turned = sem("act_turned")
    act_copied = sem("act_copied")
    down_ready = sem("down_ready")
    out_copied = sem("out_copied")
    rows_sent = sem("rows_sent")
    results_stored = [sem(f"results_stored{k}") for k in range(OR)]
    results_loaded = [sem(f"results_loaded{c}") for c in range(NC)]
    sum_ready = sem("sum_ready")
    swdge_sems = range(rows_sent.num, results_stored[-1].num + 1)
    all_sems = range(min(s.num for s in sems), max(s.num for s in sems) + 1)
    assert len(all_sems) == len(sems)

    chunks, events, _ = core_schedule()

    def group_end(g):
        return HPG * sum(TPC * (c + 1) for gg, c in chunks if gg <= g)

    pbuf = [arena[:, 8 * CH:11 * CH][:, k * 3 * CH // 2:(k + 1) * 3 * CH // 2] for k in (0, 1)]
    pbuf.append(rec[:, :, :].rearrange("p a t -> p (a t)")[:, 0:3 * CH // 2])

    def parts(i):
        return pbuf[i % PB].bitcast(BF16).rearrange("p (l t) -> p l t", l=3)

    def stored(i):
        return sum(32 if k % 2 else 16 for k in range(i % PB, i + 1, PB))

    def masks_to(j, kt):
        return TPC * j + kt - TPC * chunks[j][1] + 1

    def load_operands(sp, g, cols, done):
        b, heads, rows = g % 2, slice(g * HPG, (g + 1) * HPG), 3 * HD
        for r in range(3):
            for src, at, dst in ((qsplit, 0, qa), (ksplit, r * HD, ka)):
                sp.dma_start(dst[r * rows:(r + 1) * rows, b, :, cols],
                             src.rearrange("l (i h) t -> (l i) h t", h=H)[at:at + rows, heads, cols]
                             ).then_inc(done, 16)

    def guard_rows(b):
        return qa[64:96, b, :, :].rearrange("p h t -> p (h t)").bitcast(F32)

    def key_guard(b):
        return ka[64:96, b, :, :].rearrange("p h t -> p (h t)").bitcast(F32)

    with nc.Block() as block:

        @block.sync
        def _(sp):
            sp.dma_start(xs[:, :, :], x_in.rearrange("(t p) d -> p t d", p=128)).then_inc(x_loaded, 16)
            sp.wait_ge(x_loaded, 16)

        @block.gpsimd
        def _(pool):
            pool.memset(key_guard(1), ONES).then_inc(pool_s, 1)
            pool.wait_ge(pool_s, 1)
            n = 1
            for tile, value in ((identf, 0.0), (identb, 0.0), (mask_rows, 0.0)):
                pool.memset(tile[:, :], value).then_inc(pool_s, 1)
                n += 1
            pool.iota(revi[:, :], pattern=[[-1, E]], base=E, channel_multiplier=0).then_inc(pool_s, 1)
            pool.iota(inti[:, 0:NSLOT], pattern=[[1, NSLOT]], base=0, channel_multiplier=0).then_inc(pool_s, 1)
            pool.iota(inti[:, NSLOT:], pattern=[[128, TT]], base=0, channel_multiplier=0).then_inc(pool_s, 1)
            pool.iota(rowid[:, :, :], pattern=[[T, TOPK], [128, TT]], base=0, channel_multiplier=1).then_inc(pool_s, 1)
            pool.memset(padrow[:, :], 0.0).then_inc(pool_s, 1)
            pool.memset(below[:, :], 0.0).then_inc(pool_s, 1)
            pool.memset(ones[:, :], 1.0).then_inc(pool_s, 1)
            pool.memset(before[:, :, :], 0.0).then_inc(pool_s, 1)
            pool.wait_ge(pool_s, n + 8)
            pool.iota(padrow[:, D + 1:D + 2].bitcast(I32), pattern=[[0, 1]], base=TOPK * T,
                      channel_multiplier=1).then_inc(const_ready, 1)
            pool.affine_select(out=below[:, :], in_=below[:, :], compare_op=ALU.is_ge, fill=1.0,
                               base=0, pattern=[[-1, 128]], channel_multiplier=1).then_inc(const_ready, 1)
            pool.affine_select(out=before[:, :, :], in_=before[:, :, :], compare_op=ALU.is_ge, fill=1.0,
                               base=0, pattern=[[-1, E], [1, E]], channel_multiplier=0).then_inc(const_ready, 1)
            pool.tensor_copy(jstep[:, :], inti[:, 0:NSLOT]).then_inc(const_ready, 1)
            pool.tensor_copy(kstep[:, :], inti[:, NSLOT:]).then_inc(const_ready, 1)
            for tile in (identf, identb):
                pool.affine_select(out=tile[:, :], in_=tile[:, :], compare_op=ALU.not_equal, fill=1.0,
                                   base=0, pattern=[[-1, 128]], channel_multiplier=1).then_inc(const_ready, 1)
            pool.affine_select(out=mask_rows[:, :], in_=mask_rows[:, :], compare_op=ALU.is_ge, fill=MASKED,
                               base=0, pattern=[[-1, 128]], channel_multiplier=1).then_inc(const_ready, 1)
            pool.tensor_copy(rev[:, :], revi[:, :]).then_inc(const_ready, 1)
            pool.wait_ge(const_ready, 9)

        @block.vector
        def _(dve):
            dve.memset(vv[:, :, :, :], 1.0).then_inc(dve_s, 1)
            dve.memset(key_guard(0), ONES).then_inc(dve_s, 1)
            dve.wait_ge(dve_s, 2)

    nc.all_engine_barrier(sems_to_clear=all_sems)

    with nc.Fori(0, NLAYER) as layer:
        with nc.Block() as block:

            @block.sync
            def _(sp):
                one = bass.ds(layer, 1)
                sp.dma_start(w5s[:, :, :], w5[one].rearrange("o p w d -> (o p) w d")).then_inc(params_loaded, 16)
                sp.dma_start(b4s[:, :], b4[one].rearrange("o p w -> (o p) w")).then_inc(params_loaded, 16)
                sp.dma_start(vbc[:, :, :].rearrange("p v d -> p (v d)"),
                             vecs[one].broadcast_to([128, 4 * D])).then_inc(params_loaded, 16)
                sp.dma_start(wos[:, :], wo_w[one].rearrange("o p d -> (o p) d")).then_inc(params_loaded, 16)
                sp.dma_start(rtab, rope[one].rearrange("o p a t -> (o p) a t")).then_inc(params_loaded, 16)
                def load_first(c):
                    for i in (2 * c, 2 * c + 1):
                        sp.wait_ge(parts_stored[i % PB], stored(i))
                    load_operands(sp, 0, slice(c * CH, (c + 1) * CH), chunk_loaded[c])

                sp.wait_ge(guard_zeroed, 2)
                for c in range(NC):
                    cols = slice(c * CH, (c + 1) * CH)
                    sp.wait_ge(part2_ready, 2 * c + 1)
                    sp.dma_start(qsplit[:, :, cols].rearrange("l p t -> p l t"), parts(2 * c)).then_inc(parts_stored[2 * c % PB], 16)
                    sp.wait_ge(part2_ready, 2 * c + 2)
                    sp.dma_start(ksplit[0:3, :, cols].rearrange("l p t -> p l t"),
                                 parts(2 * c + 1)).then_inc(parts_stored[(2 * c + 1) % PB], 16)
                    sp.dma_start(ksplit[3:5, :, cols].rearrange("l p t -> p l t"),
                                 parts(2 * c + 1)[:, 0:2, :]).then_inc(parts_stored[(2 * c + 1) % PB], 16)
                    if c:
                        load_first(c - 1)
                load_first(NC - 1)
                load_operands(sp, 1, slice(0, T), group_loaded[1])

                bulk = [(rts[:, :], router), (wgs[:, :, :], w_gate.rearrange("e d m -> d e m")),
                        (wus[:, :, :], w_up.rearrange("e d m -> d e m")),
                        (wds[0:MR, :, :, :], w_down.rearrange("e (c p) d -> p e c d", p=MR))]
                for ev in events:
                    if ev[0] == "maxout":
                        j = ev[1]
                        g, c = chunks[j]
                        sp.wait_ge(guard_split, j + 1)
                        if j >= MD:
                            sp.wait_ge(guard_ready[j % MD], 16 * (j // MD))
                        sp.dma_start(guard[j % MD].rearrange("l r t -> r l t"), m3[:, j % MD, :, :]).then_inc(guard_stored[j % MD], 16)
                        sp.wait_ge(guard_stored[j % MD], 16 * (j // MD + 1))
                        sp.dma_start(qa[GUARD:GUARD + 3, g % 2, :, c * CH:(c + 1) * CH],
                                     guard[j % MD].rearrange("l (h q) t -> l h (q t)", h=HPG)).then_inc(guard_ready[j % MD], 16)
                        if BULK <= j < BULK + len(bulk):
                            dst, src = bulk[j - BULK]
                            with sp.If(layer == 0):
                                sp.dma_start(dst, src).then_inc(weights_loaded, 16)
                        elif j == BULK + len(bulk):
                            sp.dma_start(sent.rearrange("(j p) c -> p j c", p=128),
                                         padrow[:, :].rearrange("p (o c) -> p o c", o=1).broadcast_to([128, NSLOT, ROW])
                                         ).then_inc(sent_reset, 16)
                    elif ev[0] == "reload" and ev[1] + 2 < NG:
                        sp.wait_ge(guard_zeroed, ev[1] + 3)
                        load_operands(sp, ev[1] + 2, slice(0, T), group_loaded[ev[1] + 2])

                sp.wait_ge(sent_reset, 16)

            @block.vector
            def _(dve):
                n = [0]

                def link(ins):
                    n[0] += 1
                    ins.then_inc(dve_s, 1)
                    dve.wait_ge(dve_s, n[0])

                for t in range(TT):
                    ins = dve.bn_stats(stats[:, t, :], xs[:, t, :])
                link(ins)
                for t in range(TT):
                    ins = dve.bn_aggr(mv[:, t, :], stats[:, t, :])
                link(ins)
                dve.tensor_scalar(rst[:, 0, :], mv[:, :, 1], LN_EPS, None, ALU.add).then_inc(variance_ready, 1)
                dve.wait_ge(roots_ready, 1)
                link(dve.reciprocal(rst[:, 0, :], rst[:, 0, :]))
                for t in range(TT):
                    ins = dve.tensor_scalar(x1[:, t, :], xs[:, t, :], mv[:, t, 0:1], rst[:, 0, t:t + 1],
                                            ALU.subtract, ALU.mult)
                link(ins)
                for t in range(TT):
                    ins = dve.tensor_tensor_reduce(hn[:, t, :], x1[:, t, :], x1[:, t, :], 1.0, 0.0,
                                                   ALU.mult, ALU.add, rst[:, 1, t:t + 1])
                link(ins)
                dve.tensor_scalar(rst[:, 1, :], rst[:, 1, :], 1.0 / D, RMS_EPS, ALU.mult, ALU.add).then_inc(variance_ready, 1)
                dve.wait_ge(roots_ready, 2)
                link(dve.reciprocal(rst[:, 1, :], rst[:, 1, :]))
                with dve.If(layer == 1):
                    dve.memset(rst[:, 3, :], 1.0).then_inc(dve_s, 1)
                with dve.If(layer != 1):
                    dve.tensor_copy(rst[:, 3, :], rst[:, 1, :]).then_inc(dve_s, 1)
                n[0] += 1
                dve.wait_ge(dve_s, n[0])
                dve.wait_ge(params_loaded, 80)

                def norms(c):
                    for t in range(TPC * c, TPC * (c + 1)):
                        ins = dve.tensor_scalar(x1[:, t, :], xs[:, t, :], mv[:, t, 0:1], rst[:, 0, t:t + 1],
                                                ALU.subtract, ALU.mult)
                    link(ins)
                    for t in range(TPC * c, TPC * (c + 1)):
                        dve.scalar_tensor_tensor(hn[:, t, :], x1[:, t, :], rst[:, 3, t:t + 1], vbc[:, V_LN1, :],
                                                 ALU.mult, ALU.mult).then_inc(normed, 1)

                norms(0)
                norms(1)

                def remainder(i):
                    dve.wait_ge(part0_ready, i + 1)
                    dve.tensor_tensor(tmp(6 + i % 2), tmp(4 + i % 2), parts(i)[:, 0, :], ALU.subtract).then_inc(remainder_ready, 1)

                for c in range(NC):
                    cols = slice(c * CH, (c + 1) * CH)
                    for which in (0, 1):
                        i = 2 * c + which
                        if i >= 2:
                            dve.wait_ge(rotated, i - 1)
                        for k in (0, 1):
                            dve.wait_ge(projected, 2 * i + k + 1)
                            dve.scalar_tensor_tensor(tmp(2 * (i % 2) + k), ps[:, 2 + 2 * which + k, :],
                                                     b4s[:, 2 * which + k:2 * which + k + 1], rtab[:, k, cols],
                                                     ALU.add, ALU.mult).then_inc(terms_ready, 1)
                        if i:
                            if i >= 3:
                                dve.wait_ge(part2_ready, i - 2)
                            remainder(i - 1)
                    if c + 2 < NC:
                        norms(c + 2)
                    dve.wait_ge(values_projected, c + 1)
                    dve.tensor_tensor(vv[:, TPC * c:TPC * (c + 1), :, 0:HD],
                                      ps[:, 6 + c % 2, :].rearrange("p (t h d) -> p t h d", t=TPC, h=H),
                                      vbc[:, V_BV:V_BV + 1, :].rearrange("p o (h d) -> p o h d", h=H).broadcast_to(
                                          [128, TPC, H, HD]), ALU.add).then_inc(values_ready, 1)
                dve.wait_ge(part2_ready, 2 * NC - 2)
                remainder(2 * NC - 1)

                dve.wait_ge(rotated, 2 * NC)
                dve.wait_ge(values_ready, NC)
                dve.memset(ps[:, 6:8, :], 0.0).then_inc(output_zeroed, 1)
                mi = 0
                n = [0]

                def link(ins):
                    n[0] += 1
                    ins.then_inc(dve_core_s, 1)
                    dve.wait_ge(dve_core_s, n[0])

                for ev in events:
                    kind = ev[0]
                    if kind in ("rowmax", "maxout", "normalise", "turn", "project"):
                        bank = SB + mi % MB
                        mi += 1
                        dve.wait_ge(filler_ready, mi)
                    if kind == "rowmax":
                        _, j, qt, h0, some, kc, final = ev
                        g, c = chunks[j]
                        w = min(CH, (TPC * c + qt + 1) * 128 - kc * CH)
                        dve.tensor_reduce(mpart[:, j % MD, h0:h0 + some, qt, kc],
                                          ps[:, bank, 0:some * w].rearrange("p (h w) -> p h w", h=some),
                                          axis=AX.X, op=ALU.max).then_inc(filler_used, 1)
                        if final:
                            dve.wait_ge(filler_used, mi)
                            if j >= MD:
                                dve.wait_ge(guard_split, j - MD + 1)
                            dve.tensor_reduce(mx[:, j % MD, :], mpart[:, j % MD, :, :, 0:c + 1].rearrange("p h q c -> p (h q) c"), axis=AX.X,
                                              op=ALU.max, negate=True).then_inc(maxima_ready, 1)
                    elif kind == "maxout":
                        j = ev[1]
                        if j >= MD:
                            dve.wait_ge(guard_ready[j % MD], 16 * (j // MD))
                        src = ps[0:16, bank, 0:128]
                        link(dve.tensor_copy(m3[:, j % MD, 0, :], src))
                        dve.tensor_tensor(mr, src, m3[:, j % MD, 0, :], ALU.subtract).then_inc(filler_used, 1)
                        dve.wait_ge(filler_used, mi)
                        link(dve.tensor_copy(m3[:, j % MD, 1, :], mr))
                        dve.tensor_tensor(m3[:, j % MD, 2, :], mr, m3[:, j % MD, 1, :],
                                          ALU.subtract).then_inc(guard_split, 1)
                    elif kind == "normalise":
                        j = ev[1]
                        g, c = chunks[j]
                        turned = ps[:, bank, :].rearrange("p (q h r) -> p q h r", q=TPC, r=32)
                        link(dve.reciprocal(rden[:, :, :, :], turned[:, :, :, HD:HD + 1]))
                        dve.tensor_tensor(
                            onat[:, TPC * c:TPC * (c + 1), 32 * g:32 * g + 32].rearrange("p q (h i) -> p q h i", i=HD),
                            turned[:, :, :, 0:HD], rden[:, :, :, :].broadcast_to([128, TPC, HPG, HD]),
                            ALU.mult).then_inc(filler_used, 1)
                        dve.wait_ge(filler_used, mi)
                        dve.engine_nop().then_inc(output_normalised, 1)
                    elif kind == "turn":
                        c = ev[1]
                        dve.tensor_copy(hT[:, c * CH:(c + 1) * CH], ps[:, bank, :]).then_inc(filler_used, 1)
                    elif kind == "project":
                        c = ev[1]
                        rows = slice(TPC * c, TPC * (c + 1))
                        y = rec[:, 0, :].rearrange("p (t d) -> p t d", d=D)
                        dve.tensor_tensor(y, ps[:, bank, :].rearrange("p (t d) -> p t d", d=D),
                                          vbc[:, V_BO:V_BO + 1, :].broadcast_to([128, TPC, D]),
                                          ALU.add).then_inc(filler_used, 1)
                        dve.wait_ge(filler_used, mi)
                        with dve.If(layer == 1):
                            dve.tensor_tensor(xs[:, rows, :], xs[:, rows, :], y, ALU.add).then_inc(residual_added, 1)
                        with dve.If(layer != 1):
                            dve.tensor_tensor(x1[:, rows, :], x1[:, rows, :], y, ALU.add).then_inc(residual_added, 1)
                        dve.wait_ge(residual_added, c + 1)
                        for k in range(TPC):
                            t = TPC * c + k
                            ins = dve.tensor_tensor_reduce(rec[:, 1, k * D:(k + 1) * D], x1[:, t, :], x1[:, t, :],
                                                           1.0, 0.0, ALU.mult, ALU.add, rst[:, 2, t:t + 1])
                        link(ins)

            @block.gpsimd
            def _(pool):
                for b in (0, 1):
                    pool.memset(guard_rows(b), 0.0).then_inc(guard_zeroed, 1)
                pool.wait_ge(guard_zeroed, 2)

                def third(i):
                    pool.wait_ge(part1_ready, i + 1)
                    pool.tensor_tensor(parts(i)[:, 2, :], tmp(6 + i % 2), parts(i)[:, 1, :],
                                       ALU.subtract).then_inc(part2_ready, 1)

                for i in range(2 * NC):
                    pool.wait_ge(terms_ready, 2 * i + 2)
                    if i >= 2:
                        pool.wait_ge(remainder_ready, i - 1)
                    pool.tensor_tensor(tmp(4 + i % 2), tmp(2 * (i % 2)), tmp(2 * (i % 2) + 1),
                                       ALU.add).then_inc(rotated, 1)
                    if i:
                        third(i - 1)
                third(2 * NC - 1)

                pool.wait_ge(part2_ready, 2 * NC)
                for ev in events:
                    if ev[0] == "scores":
                        _, s, j, kt, h = ev
                        if kt >= TPC * chunks[j][1] and h == HPG - 1:
                            pool.wait_ge(probs_ready, HPG * (s + 1))
                            own = probs[:, s % 2, :, 0:128]
                            pool.affine_select(out=own, in_=own, compare_op=ALU.is_ge, fill=0.0, base=0,
                                               pattern=[[0, HPG], [1, 128]], channel_multiplier=-1
                                               ).then_inc(masked, 1)
                    elif ev[0] == "reload" and ev[1] + 2 < NG:
                        pool.wait_ge(scores_ready, group_end(ev[1]))
                        pool.wait_ge(masked, TPC * NC * (ev[1] + 1) + TPC)
                        pool.memset(guard_rows(ev[1] % 2), 0.0).then_inc(guard_zeroed, 1)
                        pool.wait_ge(guard_zeroed, ev[1] + 3)

            @block.scalar
            def _(act):
                act.wait_ge(variance_ready, 1)
                act.activation(rst[:, 0, :], rst[:, 0, :], ACT.Sqrt).then_inc(roots_ready, 1)
                act.wait_ge(variance_ready, 2)
                act.activation(rst[:, 1, :], rst[:, 1, :], ACT.Sqrt).then_inc(roots_ready, 1)

                def second(i):
                    act.wait_ge(remainder_ready, i + 1)
                    act.activation(parts(i)[:, 1, :], tmp(6 + i % 2), ACT.Copy).then_inc(part1_ready, 1)

                def turned(c):
                    act.wait_ge(tokens_turned, c + 1)
                    act.activation(hT[:, c * CH:(c + 1) * CH], ps[:, c % 2, :], ACT.Copy).then_inc(tokens_copied, 1)

                turned(0)
                for c in range(NC):
                    if c + 1 < NC:
                        turned(c + 1)
                    for i in (2 * c, 2 * c + 1):
                        act.wait_ge(rotated, i + 1)
                        if i >= PB:
                            act.wait_ge(parts_stored[i % PB], stored(i - PB))
                        act.activation(parts(i)[:, 0, :], tmp(4 + i % 2), ACT.Copy).then_inc(part0_ready, 1)
                        if i:
                            second(i - 1)
                second(2 * NC - 1)

                for ev in events:
                    if ev[0] == "scores":
                        _, s, j, kt, h = ev
                        g, c = chunks[j]
                        n = CH - max(0, kt - TPC * c) * 128
                        u = HPG * s + h
                        if s >= 2 and h == 0:
                            act.wait_ge(values_weighted, s - 1)
                        act.wait_ge(scores_ready, u + 1)
                        act.activation(probs[:, s % 2, h, 0:n], ps[:, u % SB, 0:n], ACT.Exp,
                                       scale=SCALE).then_inc(probs_ready, 1)
                    elif ev[0] == "evacuate":
                        j = ev[1]
                        act.wait_ge(values_weighted, sum(TPC * (c + 1) for _, c in chunks[:j + 1]))
                        if j >= 2:
                            act.wait_ge(output_normalised, j - 1)
                        act.activation(otf[:, j % 2, :], ps[:, 6 + j % 2, :], ACT.Copy).then_inc(output_copied, 1)

            @block.tensor
            def _(pe):
                def turn_tokens(c):
                    for k in range(TPC):
                        t = TPC * c + k
                        pe.wait_ge(normed, t + 1)
                        if c >= 2:
                            pe.wait_ge(tokens_copied, c - 1)
                        ins = pe.transpose(ps[:, c % 2, k * 128:(k + 1) * 128], hn[:, t, :], identf[:, :])
                    ins.then_inc(tokens_turned, 1)

                turn_tokens(0)
                for c in range(NC):
                    if c + 1 < NC:
                        turn_tokens(c + 1)
                    pe.wait_ge(tokens_copied, c + 1)
                    pe.wait_ge(params_loaded, 80)
                    for w in range(4):
                        if c:
                            pe.wait_ge(terms_ready, 4 * (c - 1) + w + 1)
                        pe.matmul(ps[:, 2 + w, :], w5s[:, w, :], hT[:, c * CH:(c + 1) * CH],
                                  start=True, stop=True).then_inc(projected, 1)
                    if c >= 2:
                        pe.wait_ge(values_ready, c - 1)
                    for k in range(TPC):
                        t = TPC * c + k
                        ins = pe.matmul(ps[:, 6 + c % 2, k * 128:(k + 1) * 128], hT[:, t * 128:(t + 1) * 128],
                                        w5s[:, W_V, :], start=True, stop=True)
                    ins.then_inc(values_projected, 1)

                pe.wait_ge(terms_ready, 4 * NC)
                pe.wait_ge(values_ready, NC)
                mi = 0
                pe.wait_ge(output_zeroed, 1)
                for ev in events:
                    kind = ev[0]
                    if kind in ("rowmax", "maxout", "normalise", "turn", "project"):
                        bank = SB + mi % MB
                        if mi >= MB:
                            pe.wait_ge(filler_used, mi - MB + 1)
                        mi += 1
                    if kind == "rowmax":
                        _, j, qt, h0, some, kc, final = ev
                        g, c = chunks[j]
                        b = g % 2
                        if qt == 0 and h0 == 0 and (kc == 0 or c == 0):
                            pe.wait_ge(group_loaded[g] if g else chunk_loaded[c], 16 * 6)
                        tile = TPC * c + qt
                        n = min(CH, (tile + 1) * 128 - kc * CH)
                        diag = kc == c
                        for k in range(some):
                            dst = ps[:, bank, k * n:(k + 1) * n]
                            ins = pe.matmul(dst, qa[0:KROWS, b, h0 + k, tile * 128:(tile + 1) * 128],
                                            ka[0:KROWS, b, h0 + k, kc * CH:kc * CH + n], start=True, stop=not diag)
                            if diag:
                                ins = pe.matmul(dst[:, n - 128:n], identb[:, :], mask_rows[:, :],
                                                start=False, stop=True)
                        ins.then_inc(filler_ready, 1)
                    elif kind == "maxout":
                        j = ev[1]
                        pe.wait_ge(maxima_ready, j + 1)
                        pe.transpose(ps[0:16, bank, 0:128], mx[:, j % MD, :], identf[:, :]).then_inc(filler_ready, 1)
                    elif kind == "normalise":
                        j = ev[1]
                        pe.wait_ge(output_copied, j + 1)
                        for k in range(TPC):
                            ins = pe.transpose(ps[:, bank, k * 128:(k + 1) * 128],
                                               otf[:, j % 2, k * 128:(k + 1) * 128], identf[:, :])
                        ins.then_inc(filler_ready, 1)
                        written = mi
                    elif kind == "turn":
                        c = ev[1]
                        pe.wait_ge(filler_used, written)
                        for k in range(TPC):
                            ins = pe.transpose(ps[:, bank, k * 128:(k + 1) * 128], onat[:, TPC * c + k, :], identf[:, :])
                        ins.then_inc(filler_ready, 1)
                        written = mi
                    elif kind == "project":
                        c = ev[1]
                        pe.wait_ge(filler_used, written)
                        for k in range(TPC):
                            t = TPC * c + k
                            ins = pe.matmul(ps[:, bank, k * 128:(k + 1) * 128], hT[:, t * 128:(t + 1) * 128],
                                            wos[:, :], start=True, stop=True)
                        ins.then_inc(filler_ready, 1)
                    elif kind == "scores":
                        _, s, j, kt, h = ev
                        g, c = chunks[j]
                        b = g % 2
                        if kt == 0 and h == 0:
                            pe.wait_ge(guard_ready[j % MD], 16 * (j // MD + 1))
                        q0 = max(0, kt - TPC * c) * 128
                        n = CH - q0
                        u = HPG * s + h
                        if u >= SB:
                            pe.wait_ge(probs_ready, u - SB + 1)
                        dst = ps[:, u % SB, 0:n]
                        pe.matmul(dst, ka[0:KROWS, b, h, kt * 128:(kt + 1) * 128],
                                  qa[0:KROWS, b, h, c * CH + q0:(c + 1) * CH],
                                  start=True, stop=True).then_inc(scores_ready, 1)
                    elif kind == "values":
                        _, s, j, kt = ev
                        g, c = chunks[j]
                        q0 = max(0, kt - TPC * c) * 128
                        pe.wait_ge(probs_ready, HPG * (s + 1))
                        if kt >= TPC * c:
                            pe.wait_ge(masked, masks_to(j, kt))
                        if kt == 0 and j >= 2:
                            pe.wait_ge(output_copied, j - 1)
                        for h in range(HPG):
                            ins = pe.matmul(ps[32 * h:32 * h + HD + 1, 6 + j % 2, q0:CH],
                                            vv[:, kt, g * HPG + h, :], probs[:, s % 2, h, 0:CH - q0],
                                            start=kt == 0, stop=kt == TPC * (c + 1) - 1)
                        ins.then_inc(values_weighted, 1)

        with nc.Block() as block:

            @block.tensor
            def _(pe):
                with pe.If(layer != 1):
                    for c in range(NC):
                        if c >= 2:
                            pe.wait_ge(h2_copied, c - 1)
                        for k in range(TPC):
                            t = TPC * c + k
                            pe.wait_ge(h2_ready, t + 1)
                            ins = pe.transpose(ps[:, 4 + c % 2, k * 128:(k + 1) * 128], pay[:, 0, t, 0:D], identf[:, :])
                        ins.then_inc(h2_turned, 1)
                    pe.wait_ge(weights_loaded, 64)
                    for t in range(TT):
                        pe.wait_ge(h2_copied, t // TPC + 1)
                        ins = pe.matmul(ps[:, 6, t * E:(t + 1) * E], hT[:, t * 128:(t + 1) * 128], rts[:, :],
                                        start=True, stop=True)
                    ins.then_inc(logits_ready, 1)
                    pe.wait_ge(taken_ready, 1)
                    taken = gw[:, 5, :, :].rearrange("p t e -> p (t e)")
                    pe.matmul(ps[:, 7, 0:TT * E], below[:, :], taken, start=True, stop=True)
                    pe.matmul(ps[:, 7, TT * E:2 * TT * E], ones[:, :], taken, start=True, stop=True).then_inc(ranks_ready, 1)

            @block.scalar
            def _(act):
                with act.If(layer != 1):
                    act.wait_ge(squares_ready, 1)
                    act.activation(rst[:, 2, :], rst[:, 2, :], ACT.Sqrt).then_inc(root_ready, 1)
                    for c in range(NC):
                        act.wait_ge(h2_turned, c + 1)
                        act.activation(hT[:, c * CH:(c + 1) * CH], ps[:, 4 + c % 2, :], ACT.Copy).then_inc(h2_copied, 1)
                    act.wait_ge(logits_shifted, 1)
                    act.activation(gw[:, 0, :, :], gw[:, 0, :, :], ACT.Exp).then_inc(logits_exp, 1)

            @block.vector
            def _(dve):
                with dve.If(layer != 1):
                    n = [0]

                    def link(ins):
                        n[0] += 1
                        ins.then_inc(dve_router_s, 1)
                        dve.wait_ge(dve_router_s, n[0])

                    dve.tensor_scalar(rst[:, 2, :], rst[:, 2, :], 1.0 / D, RMS_EPS, ALU.mult, ALU.add).then_inc(squares_ready, 1)
                    dve.wait_ge(root_ready, 1)
                    link(dve.reciprocal(rst[:, 3, :], rst[:, 2, :]))
                    for t in range(TT):
                        dve.scalar_tensor_tensor(pay[:, 0, t, 0:D], x1[:, t, :], rst[:, 3, t:t + 1], vbc[:, V_LN2, :],
                                                 ALU.mult, ALU.mult).then_inc(h2_ready, 1)
                    dve.wait_ge(logits_ready, 1)
                    lg = ps[:, 6, 0:TT * E].rearrange("p (t e) -> p t e", e=E)
                    shape = [128, TT, E]

                    def wide(k):
                        return gs[:, k, :].rearrange("p (t o) -> p t o", o=1).broadcast_to(shape)

                    revb = rev[:, :].rearrange("p (o e) -> p o e", o=1).broadcast_to(shape)
                    link(dve.tensor_reduce(gs[:, 0, :], lg, axis=AX.X, op=ALU.max))
                    dve.tensor_tensor(gw[:, 0, :, :], lg, wide(0), ALU.subtract).then_inc(logits_shifted, 1)
                    dve.wait_ge(logits_exp, 1)
                    link(dve.tensor_reduce(gs[:, 1, :], gw[:, 0, :, :], axis=AX.X, op=ALU.add))
                    link(dve.reciprocal(gs[:, 0, :], gs[:, 1, :]))
                    link(dve.tensor_tensor(gw[:, 1, :, :], gw[:, 0, :, :], wide(0), ALU.mult))
                    def pick(src, dst, peak, at):
                        link(dve.tensor_reduce(gs[:, peak, :], src, axis=AX.X, op=ALU.max))
                        link(dve.tensor_tensor(gw[:, 7, :, :], src, wide(peak), ALU.is_equal))
                        link(dve.tensor_tensor(gw[:, 7, :, :], gw[:, 7, :, :], revb, ALU.mult))
                        link(dve.tensor_reduce(gs[:, at, :], gw[:, 7, :, :], axis=AX.X, op=ALU.max))
                        link(dve.tensor_tensor(dst, revb, wide(at), ALU.is_equal))

                    pick(gw[:, 1, :, :], gw[:, 2, :, :], 2, 3)
                    link(dve.scalar_tensor_tensor(gw[:, 3, :, :], gw[:, 2, :, :], -2.0, gw[:, 1, :, :], ALU.mult, ALU.add))
                    pick(gw[:, 3, :, :], gw[:, 4, :, :], 4, 3)
                    dve.tensor_tensor(gw[:, 5, :, :], gw[:, 2, :, :], gw[:, 4, :, :], ALU.add).then_inc(taken_ready, 1)
                    link(dve.tensor_tensor(gs[:, 5, :], gs[:, 2, :], gs[:, 4, :], ALU.add))
                    link(dve.reciprocal(gs[:, 0, :], gs[:, 5, :]))
                    for k in range(TOPK):
                        dve.tensor_tensor(pay[:, k, :, D], gs[:, 2 + 2 * k, :], gs[:, 0, :], ALU.mult)
                    dve.wait_ge(ranks_ready, 1)
                    tot = gw[:, 0, :, :]
                    link(dve.tensor_copy(tot, ps[:, 7, TT * E:2 * TT * E].rearrange("p (t e) -> p t e", e=E)))
                    a, b = tot, 3
                    step = 1
                    while step < TT:
                        dst = gw[:, b, :, :]
                        dve.tensor_copy(dst[:, 0:step, :], a[:, 0:step, :])
                        link(dve.tensor_tensor(dst[:, step:TT, :], a[:, step:TT, :], a[:, 0:TT - step, :], ALU.add))
                        a, b = dst, 10 - b
                        step *= 2
                    total = a[:, TT - 1:TT, :]
                    link(dve.tensor_tensor(gw[:, 6, :, :], a, tot, ALU.subtract))
                    over = rw[:, 0:E * TT].rearrange("p (e k) -> p e k", e=E)
                    link(dve.tensor_tensor(over, total.rearrange("p o e -> p e o").broadcast_to([128, E, TT]),
                                           kstep[:, :].rearrange("p (o k) -> p o k", o=1).broadcast_to([128, E, TT]),
                                           ALU.is_gt))
                    link(dve.tensor_reduce(cnt[:, 0, :], over, axis=AX.X, op=ALU.add))
                    tri = rw[:, 0:E * E].rearrange("p (e f) -> p e f", e=E)
                    link(dve.tensor_tensor(tri, cnt[:, 0:1, :].broadcast_to([128, E, E]), before[:, :, :], ALU.mult))
                    link(dve.tensor_reduce(cnt[:, 1, :], tri, axis=AX.X, op=ALU.add))
                    link(dve.tensor_tensor(cnt[:, 2, :], cnt[:, 0, :], cnt[:, 1, :], ALU.add))
                    past = rw[:, 0:NSLOT * E].rearrange("p (j e) -> p j e", e=E)
                    link(dve.tensor_tensor(past, jstep[:, :].rearrange("p (j o) -> p j o", o=1).broadcast_to([128, NSLOT, E]),
                                           cnt[:, 2:3, :].broadcast_to([128, NSLOT, E]), ALU.is_ge))
                    link(dve.tensor_reduce(etf[:, :], past, axis=AX.X, op=ALU.add))
                    dve.tensor_scalar(eti[:, :], etf[:, :], float(E - 1), None, ALU.min)
                    link(dve.tensor_scalar(cnt[:, 3, :], cnt[:, 1, :], 128.0, None, ALU.mult))
                    link(dve.tensor_tensor(gw[:, 6, :, :], gw[:, 6, :, :], cnt[:, 3:4, :].broadcast_to([128, TT, E]), ALU.add))
                    link(dve.tensor_tensor(gw[:, 6, :, :], gw[:, 6, :, :],
                                           ps[:, 7, 0:TT * E].rearrange("p (t e) -> p t e", e=E), ALU.add))
                    link(dve.tensor_tensor(gw[:, 3, :, :], gw[:, 6, :, :], gw[:, 2, :, :], ALU.mult))
                    link(dve.tensor_tensor(gw[:, 7, :, :], gw[:, 6, :, :], gw[:, 4, :, :], ALU.mult))
                    dve.tensor_reduce(posf[:, 0, :], gw[:, 3, :, :], axis=AX.X, op=ALU.add)
                    link(dve.tensor_reduce(posf[:, 1, :], gw[:, 7, :, :], axis=AX.X, op=ALU.add))
                    link(dve.tensor_copy(posi[:, :, :], posf[:, :, :]))

            @block.gpsimd
            def _(pool):
                with pool.If(layer != 1):
                    pool.wait_ge(h2_ready, TT)
                    for k in range(TOPK):
                        pool.tensor_copy(pay[:, k, :, D + 1].bitcast(I32), rowid[:, k, :])
                    pool.tensor_copy(pay[:, 1, :, 0:D], pay[:, 0, :, 0:D])

        with nc.Block() as block:

            @block.gpsimd
            def _(pool):
                with pool.If(layer != 1):
                    for k in range(TOPK):
                        for t in range(TT):
                            pool.indirect_dma_start(sent, bass.IndirectOffsetOnAxis(ap=posi[:, k, t:t + 1], axis=0),
                                                    pay[:, k, t, :], None).then_inc(rows_sent, 16)
                    for u in range(NSLOT):
                        pool.wait_ge(out_copied, u + 1)
                        pool.indirect_dma_start(
                            results,
                            bass.IndirectOffsetOnAxis(ap=xring[:, u % XR, D + 1:D + 2].bitcast(I32), axis=0),
                            obuf[:, u % OR, :], None, bounds_check=TOPK * T - 1,
                            oob_is_err=False).then_inc(results_stored[u % OR], 16)
                    pool.wait_ge(rows_sent, 16 * TOPK * TT)
                    for k in range(OR):
                        pool.wait_ge(results_stored[k], 16 * len(range(k, NSLOT, OR)))
                    pool.dma_reset(swdge_sems)

            @block.sync
            def _(sp):
                with sp.If(layer != 1):
                    sp.wait_ge(rows_sent, 16 * TOPK * TT)
                    for u in range(NSLOT):
                        if u >= XR:
                            v = u - XR
                            sp.wait_ge(results_stored[v % OR], 16 * (v // OR + 1))
                        sp.dma_start(xring[:, u % XR, :], sent[u * 128:(u + 1) * 128, :]).then_inc(tile_loaded[u % XR], 16)
                    for k in range(OR):
                        sp.wait_ge(results_stored[k], 16 * len(range(k, NSLOT, OR)))
                    for c in range(NC):
                        for k in range(TOPK):
                            rows = slice(k * T + c * CH, k * T + (c + 1) * CH)
                            sp.dma_start(arena[:, rows].rearrange("p (t d) -> p t d", d=D),
                                         results[rows, :].rearrange("(t p) d -> p t d", p=128)
                                         ).then_inc(results_loaded[c], 16)

            @block.tensor
            def _(pe):
                def turn(u):
                    pe.wait_ge(tile_loaded[u % XR], 16 * (u // XR + 1))
                    if u:
                        pe.wait_ge(tile_copied, u)
                    pe.transpose(ps[:, 7, 0:128], xring[:, u % XR, 0:D], identf[:, :]).then_inc(tile_turned, 1)

                with pe.If(layer != 1):
                    turn(0)
                    experts = []
                    for i in range(NSLOT + 2):
                        if i + 1 < NSLOT:
                            turn(i + 1)
                        if i < NSLOT:
                            expert = pe.value_load(eti[0:1, i:i + 1], min_val=0, max_val=E - 1)
                            experts.append(expert)
                            pe.wait_ge(tile_copied, i + 1)
                            if i >= 2:
                                pe.wait_ge(act_ready, i - 1)
                            for k, w in ((0, wgs), (1, wus)):
                                pe.matmul(ps[:, 2 * (i % 2) + k, 0:M], xt[:, i % 2, :],
                                          w[:, bass.ds(expert, 1), :].rearrange("p o m -> p (o m)"),
                                          start=True, stop=True).then_inc(gate_up_ready, 1)
                        if 1 <= i <= NSLOT:
                            u = i - 1
                            pe.wait_ge(act_ready, u + 1)
                            if u >= 2:
                                pe.wait_ge(act_copied, u - 1)
                            for k in range(MC):
                                ins = pe.transpose(ps[0:MR, 4 + u % 2, k * 128:(k + 1) * 128],
                                                   acb[u % 2][:, k * MR:(k + 1) * MR], identf[:, :])
                            ins.then_inc(act_turned, 1)
                        if i >= 2:
                            u = i - 2
                            pe.wait_ge(act_copied, u + 1)
                            if u:
                                pe.wait_ge(out_copied, u)
                            for k in range(MC):
                                ins = pe.matmul(ps[:, 6, 0:D], atb[u % 2][:, k, :],
                                                wds[0:MR, bass.ds(experts[u], 1), k, :].rearrange("p o d -> p (o d)"),
                                                start=k == 0, stop=k == MC - 1)
                            ins.then_inc(down_ready, 1)

            @block.scalar
            def _(act):
                def copy_turned(u):
                    act.wait_ge(tile_turned, u + 1)
                    if u >= 2:
                        act.wait_ge(gate_up_ready, 2 * (u - 1))
                    act.activation(xt[:, u % 2, :], ps[:, 7, 0:128], ACT.Copy).then_inc(tile_copied, 1)

                with act.If(layer != 1):
                    copy_turned(0)
                    for i in range(NSLOT + 1):
                        if i + 1 < NSLOT:
                            copy_turned(i + 1)
                        if i < NSLOT:
                            act.wait_ge(gate_up_ready, 2 * i + 1)
                            if i >= 2:
                                act.wait_ge(act_ready, i - 1)
                            act.activation(sgb[i % 2], ps[:, 2 * (i % 2), 0:M], ACT.Silu).then_inc(silu_ready, 1)
                        if i:
                            u = i - 1
                            act.wait_ge(act_turned, u + 1)
                            if u >= 2:
                                act.wait_ge(down_ready, u - 1)
                            act.activation(atb[u % 2], ps[0:MR, 4 + u % 2, :].rearrange("p (c t) -> p c t", c=MC),
                                           ACT.Copy).then_inc(act_copied, 1)

            @block.vector
            def _(dve):
                with dve.If(layer != 1):
                    for i in range(NSLOT + 2):
                        if i < NSLOT:
                            dve.wait_ge(tile_loaded[i % XR], 16 * (i // XR + 1))
                            dve.wait_ge(silu_ready, i + 1)
                            dve.wait_ge(gate_up_ready, 2 * i + 2)
                            if i >= 2:
                                dve.wait_ge(act_turned, i - 1)
                            dve.scalar_tensor_tensor(acb[i % 2], sgb[i % 2], xring[:, i % XR, D:D + 1],
                                                     ps[:, 2 * (i % 2) + 1, 0:M], ALU.mult, ALU.mult).then_inc(act_ready, 1)
                        if i >= 2:
                            u = i - 2
                            dve.wait_ge(down_ready, u + 1)
                            if u >= OR:
                                dve.wait_ge(results_stored[u % OR], 16 * (u // OR))
                            dve.tensor_copy(obuf[:, u % OR, :], ps[:, 6, 0:D]).then_inc(out_copied, 1)
                    n = 0
                    for c in range(NC):
                        dve.wait_ge(results_loaded[c], 16 * TOPK)
                        x1c = x1[:, TPC * c:TPC * (c + 1), :].rearrange("p t d -> p (t d)")
                        xsc = xs[:, TPC * c:TPC * (c + 1), :].rearrange("p t d -> p (t d)")
                        for k in range(TOPK):
                            dve.tensor_tensor(x1c, x1c, arena[:, k * T + c * CH:k * T + (c + 1) * CH],
                                              ALU.add).then_inc(sum_ready, 1)
                            n += 1
                            dve.wait_ge(sum_ready, n)
                        dve.scalar_tensor_tensor(xsc, x1c, 0.5, xsc, ALU.mult, ALU.add)

        nc.all_engine_barrier(sems_to_clear=all_sems)

    with nc.Block() as block:

        @block.sync
        def _(sp):
            sp.dma_start(out.rearrange("(t p) d -> p t d", p=128), xs[:, :, :]).then_inc(x_loaded, 16)
            sp.wait_ge(x_loaded, 16)


def rotary_tables():
    i = np.arange(HD // 2, dtype=np.float32)
    pos = np.arange(T, dtype=np.float32)
    ffn = pos[:, None] * (np.float32(1.0) / np.float32(10000.0) ** (2 * i / np.float32(HD)))[None, :]
    att = pos[:, None] * (np.float32(10000.0) ** (np.float32(-2.0) * i / np.float32(HD)))[None, :]
    tabs = []
    for angle, sign in ((ffn, -1.0), (att, 1.0), (ffn, -1.0)):
        angle = angle.astype(np.float32)
        cos, sin = np.cos(angle), np.sin(angle)
        c8 = np.concatenate([cos, cos], 1).T
        s8 = np.concatenate([np.float32(sign) * sin, sin], 1).T
        tabs.append(np.stack([np.repeat(c8, H, 0), np.repeat(s8, H, 0)], 1))
    return np.ascontiguousarray(np.stack(tabs).astype(np.float32))


def kernel(**inputs):
    import concourse.bacc as bacc
    from concourse.bass_utils import run_bass_kernel_spmd as run

    v = {k: np.asarray(a) for k, a in inputs.items()}
    f = "L0_ffn_"
    a = "L0_attn_"
    other_half = np.arange(H * HD).reshape(H, 2, HD // 2)[:, ::-1, :].reshape(-1)
    rep = H // (v[f + "wk"].shape[1] // HD)

    def heads(w):
        return np.repeat(w.reshape(D, -1, HD), rep, axis=1).reshape(D, H * HD)

    fq, fk, fv = v[f + "wq"], heads(v[f + "wk"]), heads(v[f + "wv"])
    ffn5 = np.stack([fq, fq[:, other_half], fk, fk[:, other_half], fv], 1)
    aq, ak, av = v[a + "Wq"].T, v[a + "Wk"].T, v[a + "Wv"].T
    att5 = np.stack([aq, aq, ak, ak, av], 1)
    zero, one = np.zeros(D, np.float32), np.ones(D, np.float32)
    b_ffn = np.stack([zero] * 4, 1)
    b_att = np.stack([v[a + "bq"], v[a + "bq"], v[a + "bk"], v[a + "bk"]], 1)
    v_ffn = np.concatenate([v[f + "ln1_w"], zero, zero, v[f + "ln2_w"]])
    v_att = np.concatenate([one, v[a + "bv"], v[a + "bo"], one])

    wo_f, wo_a = v[f + "wo"], v[a + "Wo"].T
    by_dim = np.arange(H * HD).reshape(H, HD).T.reshape(-1)

    def turned(w):
        return np.concatenate([w[:, :4][:, :, by_dim], w[:, 4:]], 1)

    ffn5, att5, b_att = turned(ffn5), turned(att5), b_att[by_dim]
    arrays = {
        "x_in": v[a + "x"].reshape(T, D),
        "w5": np.stack([ffn5, att5, ffn5]),
        "b4": np.stack([b_ffn, b_att, b_ffn]),
        "vecs": np.stack([v_ffn, v_att, v_ffn]),
        "wo_w": np.stack([wo_f, wo_a, wo_f]),
        "rope": rotary_tables(),
        "router": v[f + "router_w"],
        "w_gate": v[f + "w_gate"],
        "w_up": v[f + "w_up"],
        "w_down": v[f + "w_down"],
    }
    arrays = {k: np.ascontiguousarray(b) for k, b in arrays.items()}
    nc = bacc.Bacc("TRN2", target_bir_lowering=False, num_devices=1)
    args = [nc.dram_tensor(k, b.shape, mybir.dt.from_np(b.dtype), kind="ExternalInput").ap() for k, b in arrays.items()]
    out = nc.dram_tensor("out", (T, D), F32, kind="ExternalOutput").ap()
    macaron_kernel(nc, *args, out)
    r = run(nc, [arrays], core_ids=[0])
    return r.results[0]["out"].reshape(1, T, D)
```
